# Optimizing a Trainium2 kernel written in Bass

```python
import numpy as np
import jax
import jax.numpy as jnp

def _softmax(x, axis=-1):
    return jax.nn.softmax(x, axis=axis)

def _gelu(x):
    return jax.nn.gelu(x, approximate=True)

def _silu(x):
    return jax.nn.silu(x)

def _sigmoid(x):
    return jax.nn.sigmoid(x)

def _layernorm(x, axis=-1, eps=1e-05):
    m = jnp.mean(x, axis=axis, keepdims=True)
    v = jnp.var(x, axis=axis, keepdims=True)
    return (x - m) / jnp.sqrt(v + eps)

def _scatter_add(tgt, idx, src, axis=0):
    return tgt.at[idx].add(src)

def _segment_sum(src, seg, n):
    return jax.ops.segment_sum(src, seg, n)
kernel_name = 'mk_lm_tower_d1_tok_ids512_r4_0ba816'

def setup_inputs(seed: int=0):
    np.random.seed(seed)
    _w = jnp.asarray

    def _rec_inputs():
        import jax
        import jax.numpy as jnp
        _rk = jax.random.key(seed)
        x = jax.random.randint(jax.random.fold_in(_rk, 1), (8, 1024), 0, 12564, jnp.int32)
        return x
    x = _rec_inputs()

    def _L0_tok_setup():
        import jax, jax.numpy as jnp
        import numpy as np
        VOCAB = 50257
        EMBED = 128
        key = jax.random.key(seed)
        k1, k2 = jax.random.split(key)
        x = jax.random.randint(k1, (8, 512), 0, VOCAB, dtype=jnp.int64 if jax.config.jax_enable_x64 else jnp.int32)
        w = jax.random.normal(k2, (VOCAB, EMBED), dtype=jnp.float32)
        return {'x': x, 'w': w}
    _L0_tok_all = _L0_tok_setup()
    _L0_tok_in = {k: v for k, v in _L0_tok_all.items() if k in ('w',)}
    del _L0_tok_all

    def _L0_attn_setup():
        import jax, jax.numpy as jnp
        import numpy as np
        NHEAD = 8
        WINDOW = 64

        def _sliding_window_attention(q, k, v, w):
            B, H, S, D = q.shape
            assert S % w == 0
            nb = S // w
            qb = q.reshape(B, H, nb, w, D)
            kb = k.reshape(B, H, nb, w, D)
            vb = v.reshape(B, H, nb, w, D)
            k_prev = jnp.pad(kb, ((0, 0), (0, 0), (1, 0), (0, 0), (0, 0)))[:, :, :nb]
            v_prev = jnp.pad(vb, ((0, 0), (0, 0), (1, 0), (0, 0), (0, 0)))[:, :, :nb]
            k2 = jnp.concatenate([k_prev, kb], axis=3)
            v2 = jnp.concatenate([v_prev, vb], axis=3)
            scores = jnp.einsum('bhnqd,bhnkd->bhnqk', qb, k2) / jnp.sqrt(jnp.asarray(D, q.dtype))
            qi = jnp.arange(w)[:, None]
            ki = jnp.arange(2 * w)[None, :]
            valid = (ki >= qi + 1) & (ki <= qi + w)
            n_idx = jnp.arange(nb)[:, None, None]
            valid = valid[None] & ((n_idx > 0) | (ki[None] >= w))
            neg = jnp.asarray(-1e+30, scores.dtype)
            scores = jnp.where(valid[None, None], scores, neg)
            attn = jax.nn.softmax(scores, axis=-1)
            out = jnp.einsum('bhnqk,bhnkd->bhnqd', attn, v2)
            return out.reshape(B, H, S, D)
        key = jax.random.key(seed)
        ks = jax.random.split(key, 5)
        B, S, Dm = (2, 2048, 128)
        x = jax.random.normal(ks[0], (B, S, Dm), jnp.float32)
        w_scale = 0.02
        Wq = jax.random.normal(ks[1], (Dm, Dm), jnp.float32) * w_scale
        Wk = jax.random.normal(ks[2], (Dm, Dm), jnp.float32) * w_scale
        Wv = jax.random.normal(ks[3], (Dm, Dm), jnp.float32) * w_scale
        Wo = jax.random.normal(ks[4], (Dm, Dm), jnp.float32) * w_scale
        return {'x': x, 'Wq': Wq, 'Wk': Wk, 'Wv': Wv, 'Wo': Wo}
    _L0_attn_all = _L0_attn_setup()
    _L0_attn_in = {k: v for k, v in _L0_attn_all.items() if k in ('Wq', 'Wk', 'Wv', 'Wo')}
    del _L0_attn_all

    def _L0_ffn_setup():
        import jax, jax.numpy as jnp
        import numpy as np
        E = 64
        K = 2
        D = 128
        H = 64
        NSH = 2
        ROUTE_SCALE = 2.5
        CAP = 256
        STD = 0.02
        key = jax.random.key(seed)
        ks = jax.random.split(key, 8)
        x = jax.random.normal(ks[0], (4, 512, D), dtype=jnp.float32)
        gate_w = jax.random.normal(ks[1], (E, D), dtype=jnp.float32) * STD
        w1 = jax.random.normal(ks[2], (E, D, H), dtype=jnp.float32) * STD
        w3 = jax.random.normal(ks[3], (E, D, H), dtype=jnp.float32) * STD
        w2 = jax.random.normal(ks[4], (E, H, D), dtype=jnp.float32) * STD
        sw1 = jax.random.normal(ks[5], (D, H * NSH), dtype=jnp.float32) * STD
        sw3 = jax.random.normal(ks[6], (D, H * NSH), dtype=jnp.float32) * STD
        sw2 = jax.random.normal(ks[7], (H * NSH, D), dtype=jnp.float32) * STD
        return {'x': x, 'gate_w': gate_w, 'w1': w1, 'w3': w3, 'w2': w2, 'sw1': sw1, 'sw3': sw3, 'sw2': sw2}
    _L0_ffn_all = _L0_ffn_setup()
    _L0_ffn_in = {k: v for k, v in _L0_ffn_all.items() if k in ('gate_w', 'w1', 'w3', 'w2', 'sw1', 'sw3', 'sw2')}
    del _L0_ffn_all
    return {'x': x, 'L0_tok_w': _L0_tok_in['w'], 'L0_attn_Wq': _L0_attn_in['Wq'], 'L0_attn_Wk': _L0_attn_in['Wk'], 'L0_attn_Wv': _L0_attn_in['Wv'], 'L0_attn_Wo': _L0_attn_in['Wo'], 'L0_ffn_gate_w': _L0_ffn_in['gate_w'], 'L0_ffn_w1': _L0_ffn_in['w1'], 'L0_ffn_w3': _L0_ffn_in['w3'], 'L0_ffn_w2': _L0_ffn_in['w2'], 'L0_ffn_sw1': _L0_ffn_in['sw1'], 'L0_ffn_sw3': _L0_ffn_in['sw3'], 'L0_ffn_sw2': _L0_ffn_in['sw2']}

def reference(x, L0_tok_w, L0_attn_Wq, L0_attn_Wk, L0_attn_Wv, L0_attn_Wo, L0_ffn_gate_w, L0_ffn_w1, L0_ffn_w3, L0_ffn_w2, L0_ffn_sw1, L0_ffn_sw3, L0_ffn_sw2):
    import jax
    import jax.numpy as jnp

    def _L0_tok_ref(x, w):
        import jax, jax.numpy as jnp
        import numpy as np
        VOCAB = 50257
        EMBED = 128
        return jnp.take(w, x, axis=0)

    def _L0_attn_ref(x, Wq, Wk, Wv, Wo):
        import jax, jax.numpy as jnp
        import numpy as np
        NHEAD = 8
        WINDOW = 64

        def _sliding_window_attention(q, k, v, w):
            B, H, S, D = q.shape
            assert S % w == 0
            nb = S // w
            qb = q.reshape(B, H, nb, w, D)
            kb = k.reshape(B, H, nb, w, D)
            vb = v.reshape(B, H, nb, w, D)
            k_prev = jnp.pad(kb, ((0, 0), (0, 0), (1, 0), (0, 0), (0, 0)))[:, :, :nb]
            v_prev = jnp.pad(vb, ((0, 0), (0, 0), (1, 0), (0, 0), (0, 0)))[:, :, :nb]
            k2 = jnp.concatenate([k_prev, kb], axis=3)
            v2 = jnp.concatenate([v_prev, vb], axis=3)
            scores = jnp.einsum('bhnqd,bhnkd->bhnqk', qb, k2) / jnp.sqrt(jnp.asarray(D, q.dtype))
            qi = jnp.arange(w)[:, None]
            ki = jnp.arange(2 * w)[None, :]
            valid = (ki >= qi + 1) & (ki <= qi + w)
            n_idx = jnp.arange(nb)[:, None, None]
            valid = valid[None] & ((n_idx > 0) | (ki[None] >= w))
            neg = jnp.asarray(-1e+30, scores.dtype)
            scores = jnp.where(valid[None, None], scores, neg)
            attn = jax.nn.softmax(scores, axis=-1)
            out = jnp.einsum('bhnqk,bhnkd->bhnqd', attn, v2)
            return out.reshape(B, H, S, D)
        B, S, Dm = x.shape
        hd = Dm // NHEAD
        q = (x @ Wq.T).reshape(B, S, NHEAD, hd).transpose(0, 2, 1, 3)
        k = (x @ Wk.T).reshape(B, S, NHEAD, hd).transpose(0, 2, 1, 3)
        v = (x @ Wv.T).reshape(B, S, NHEAD, hd).transpose(0, 2, 1, 3)
        attn = _sliding_window_attention(q, k, v, WINDOW)
        attn = attn.transpose(0, 2, 1, 3).reshape(B, S, Dm)
        return attn @ Wo.T

    def _L0_ffn_ref(x, gate_w, w1, w3, w2, sw1, sw3, sw2):
        import jax, jax.numpy as jnp
        import numpy as np
        E = 64
        K = 2
        D = 128
        H = 64
        NSH = 2
        ROUTE_SCALE = 2.5
        CAP = 256
        STD = 0.02
        bs, slen, d = x.shape
        xf = x.reshape(-1, d)
        logits = xf @ gate_w.T
        scores = jax.nn.sigmoid(logits.astype(jnp.float32))
        top_scores, top_idx = jax.lax.top_k(scores, K)
        top_scores = top_scores / (top_scores.sum(-1, keepdims=True) + 1e-20)
        top_scores = top_scores * ROUTE_SCALE
        flat_e = top_idx.reshape(-1)
        x_pairs = jnp.repeat(xf, K, axis=0)
        oh = jax.nn.one_hot(flat_e, E, dtype=jnp.int32)
        pos = jnp.take_along_axis(jnp.cumsum(oh, axis=0), flat_e[:, None], axis=1)[:, 0] - 1
        buf = jnp.zeros((E, CAP, d), dtype=xf.dtype).at[flat_e, pos].set(x_pairs, mode='drop')
        h = jax.nn.silu(jnp.einsum('ecd,edh->ech', buf, w1)) * jnp.einsum('ecd,edh->ech', buf, w3)
        y = jnp.einsum('ech,ehd->ecd', h, w2)
        valid = (pos < CAP)[:, None]
        y_pairs = jnp.where(valid, y[flat_e, jnp.minimum(pos, CAP - 1)], 0.0)
        routed = (y_pairs.reshape(-1, K, d) * top_scores[..., None].astype(xf.dtype)).sum(axis=1)
        shared = jax.nn.silu(xf @ sw1) * (xf @ sw3) @ sw2
        return (shared + routed).reshape(bs, slen, d)
    h = _L0_tok_ref(x, L0_tok_w)
    h = h + _L0_attn_ref(_layernorm(h, axis=-1), L0_attn_Wq, L0_attn_Wk, L0_attn_Wv, L0_attn_Wo)
    h = h + _L0_ffn_ref(_layernorm(h, axis=-1), L0_ffn_gate_w, L0_ffn_w1, L0_ffn_w3, L0_ffn_w2, L0_ffn_sw1, L0_ffn_sw3, L0_ffn_sw2)
    return h

_drawn_inputs = setup_inputs


def setup_inputs(seed=0):
    import zlib

    import numpy as np

    out = dict(_drawn_inputs(seed))
    spreads = {}
    factors = {'L0_attn_Wq': 8.0,
     'L0_attn_Wk': 8.0,
     'L0_attn_Wv': 7.872,
     'L0_attn_Wo': 7.746,
     'L0_ffn_gate_w': 8.0,
     'L0_ffn_w1': 8.0,
     'L0_ffn_w3': 8.0,
     'L0_ffn_w2': 8.0,
     'L0_ffn_sw1': 8.0,
     'L0_ffn_sw3': 8.0,
     'L0_ffn_sw2': 8.0}
    for name, (base, spread) in spreads.items():
        noise = np.random.default_rng([zlib.crc32(name.encode()), seed]).standard_normal(out[name].shape)
        drawn = base * np.exp(spread * noise) if base else spread * noise
        out[name] = jnp.asarray(drawn.astype(out[name].dtype))
    for name, factor in factors.items():
        out[name] = (out[name] * factor).astype(out[name].dtype)
    return out
```

```python
from contextlib import ExitStack

import concourse.bass as bass
from concourse import mybir

F32, BF16, I32, U32 = mybir.dt.float32, mybir.dt.bfloat16, mybir.dt.int32, mybir.dt.uint32
ALU = mybir.AluOpType
ACT = mybir.ActivationFunctionType
AX = mybir.AxisListType

P = 128
HEADS, HD = 8, 16
PAIRS = HEADS // 2
W = 64
EPS = 1e-5
SCALE = HD ** -0.5
NEG = -1e30
CAP, ROUTE_SCALE = 256, 2.5
DEPTH = 4
HEAD_ROUNDS, TAIL_ROUNDS = 3, 3

GATHER, NORM1, PROJ, SCORE, VALUE, _, OUTP, NORM2, GATE, ROUTE, SCATTER = range(11)


def lm_tower(nc, x, tok_w, Wq, Wk, Wv, Wo, gate_w, w1, w3, w2, sw1, sw3, sw2, out):
    BATCH, SEQ = x.shape
    E, D, H = w1.shape
    TILES = BATCH * SEQ // P
    SEQ_TILES = SEQ // P
    LOOPS = TILES // DEPTH - HEAD_ROUNDS
    EPAIRS = E // 2
    SLOTS = E * CAP
    VW = 2 * HD + 1
    assert D == P and SEQ_TILES % 8 == 0 and 2 * H == P and E == W

    out_rows = out.rearrange("b s d -> (b s) d")
    xslots = nc.dram_tensor("xslots", [SLOTS, D], F32, kind="Internal").ap()
    yslots = nc.dram_tensor("yslots", [SLOTS + 1, D], F32, kind="Internal").ap()

    ctx = ExitStack()
    with ctx:
        def sb(name, shape, dt=F32):
            return ctx.enter_context(nc.sbuf_tensor(name, shape, dt))

        def sem(name):
            return ctx.enter_context(nc.semaphore(name))

        ident = sb("ident", [P, P])
        identb = sb("identb", [P, P], BF16)
        fold2 = sb("fold2", [P, W])
        before = sb("before", [P, P], BF16)
        count = sb("count", [P, E], BF16)
        onesb = sb("onesb", [P, P], BF16)
        masks = sb("masks", [P, 3 * P], BF16)
        rowmask = sb("rowmask", [P, 2])
        expert_no = sb("expert_no", [P, E])
        expert_noi = sb("expert_noi", [P, E], I32)
        neghalf = sb("neghalf", [P, 2])
        epscol = sb("epscol", [P, 2])
        zeros = sb("zeros", [P, 1024])
        raw = sb("raw", [P, 4, P])
        wo_perm = sb("wo_perm", [P, P])
        raw_gate = sb("raw_gate", [E, P])
        WqT, WkT, WvT, WoT = (sb(n, [P, P]) for n in ("WqT", "WkT", "WvT", "WoT"))
        gateT = sb("gateT", [P, E])
        shared13 = sb("shared13", [P, 2, P])
        shared2 = sb("shared2", [P, P])
        ids_i = sb("ids_i", [TILES, P], I32)
        ids_f = sb("ids_f", [TILES, P])
        idsT = sb("idsT", [P, TILES])

        hres = sb("hres", [P, TILES * P])
        x2T_all = sb("x2T_all", [P, TILES * P])
        slot_all = sb("slot_all", [P, 2 * TILES], I32)
        gain_all = sb("gain_all", [P, 2 * TILES])

        row_id = sb("row_id", [P, DEPTH], I32)
        hg = sb("hg", [P, DEPTH, P])
        st1, st2 = sb("st1", [P, 6]), sb("st2", [P, 6])
        mv = sb("mv", [P, 2, 2, 2])
        rs = sb("rs", [P, 2, 2, 2])
        xn = sb("xn", [P, 2, P])
        xnT = sb("xnT", [P, W + 2 * P])
        KT = sb("KT", [P, W + 2 * P])
        QT = sb("QT", [P, 2, 2, 2, W])
        V = sb("V", [P, DEPTH, 2, PAIRS * VW])
        mx, nmx = sb("mx", [P, 2, PAIRS, 2]), sb("nmx", [P, 2, PAIRS, 2])
        prob = sb("prob", [P, 2, 2, PAIRS * P])
        probT = sb("probT", [P, 2, PAIRS * P])
        rsum = sb("rsum", [P, 2, 2 * PAIRS])
        attn = sb("attn", [P, 2, 2, P])
        mixT = sb("mixT", [P, 2, 2, P])
        x2 = sb("x2", [P, DEPTH, P])
        elog = sb("elog", [P, 2, E])
        negd = sb("negd", [P, E])
        negs = sb("negs", [P, 2])
        top = sb("top", [P, 8])
        topi = sb("topi", [P, 8], U32)
        idx = sb("idx", [P, 2, 2])
        pick = sb("pick", [P, 2, 2, E], BF16)
        tsum, trec = sb("tsum", [P, 1]), sb("trec", [P, 1])
        rank = sb("rank", [P, 2, E])
        pos, over, slotf = sb("pos", [P, 2]), sb("over", [P, 2]), sb("slotf", [P, 2])
        slot = sb("slot", [P, DEPTH, 2], I32)

        xs = sb("xs", [P, DEPTH, 4 * P])
        w13 = sb("w13", [P, DEPTH, 2, 2, H])
        w2s = sb("w2s", [P, DEPTH, P])
        xsT = sb("xsT", [P, 2, 4 * P])
        silu = sb("silu", [P, 2, 4, H])
        hid = sb("hid", [P, 2, 2, 2, H])
        hidT = sb("hidT", [P, 2, 2 * P])
        ys = sb("ys", [P, DEPTH, 4 * P])

        ysel = sb("ysel", [P, 2 * DEPTH, 2, P])
        slot_next = sb("slot_next", [P, 2, 2 * DEPTH], I32)
        slot_now = sb("slot_now", [P, 2, 2 * DEPTH], I32)
        zero_i = sb("zero_i", [P, 2 * DEPTH], I32)
        gate_scratch = sb("gate_scratch", [P, 1])
        silu3 = [xsT[:, 0, :], xsT[:, 1, :]]
        hT3 = [prob[:, 0, 0, :], prob[:, 0, 1, :]]
        acc = [prob[:, 1, 0, :], prob[:, 1, 1, :]]

        ps = ctx.enter_context(nc.psum_tensor("ps", [P, 8, 512], F32))

        def S(pair):
            return ps[:, pair, 0:2 * P]

        def PT(blk):
            return ps[:, 4 + blk, :]

        p_v = ps[:, 4, 0:2 * P]
        p_xT, p_mix = ps[:, 6, 0:P], ps[:, 6, P:3 * P]
        p_fold, p_x2T = ps[:, 6, P:2 * P], ps[:, 6, 2 * P:3 * P]
        p_q, p_k, p_log = ps[:, 6, 0:P], ps[:, 6, P:2 * P], ps[:, 6, 2 * P:2 * P + E]
        p_wo, p_rank = ps[:, 7, 0:P], ps[:, 7, P:P + E]
        p_o = ps[:, 7, 0:2 * PAIRS * VW]

        consts_ready = sem("consts_ready")
        pool_setup = sem("pool_setup")
        dve_setup = sem("dve_setup")
        weights_in = sem("weights_in")
        ids_in = sem("ids_in")
        shared_in = sem("shared_in")
        setup_T = sem("setup_T")
        zeroed = sem("zeroed")
        id_picked = sem("id_picked")
        gathered = [sem(f"gathered{r}") for r in range(DEPTH)]
        res_saved = [sem(f"res_saved{r}") for r in range(DEPTH)]
        ln1, rstd, xn_ready = sem("ln1"), sem("rstd"), sem("xn_ready")
        xT_done, xT_ready = sem("xT_done"), sem("xT_ready")
        qk_done, qk_ready = sem("qk_done"), sem("qk_ready")
        v_done, v_ready = sem("v_done"), sem("v_ready")
        s_done, max_done, max_ready = sem("s_done"), sem("max_done"), sem("max_ready")
        p_ready, pT_done, pT_ready = sem("p_ready"), sem("pT_done"), sem("pT_ready")
        o_done, rsum_ready, attn_ready = sem("o_done"), sem("rsum_ready"), sem("attn_ready")
        fold_done, mix_ready = sem("fold_done"), sem("mix_ready")
        wo_done, res_ready = sem("wo_done"), sem("res_ready")
        ln2, x2_ready = sem("ln2"), sem("x2_ready")
        x2T_done, counted = sem("x2T_done"), sem("counted")
        x2T_saved = [sem(f"x2T_saved{b}") for b in range(2)]
        log_done, elog_ready = sem("log_done"), sem("elog_ready")
        picking = sem("picking")
        rank_done, rank_read, ranking = sem("rank_done"), sem("rank_read"), sem("ranking")
        scattered = [sem(f"scattered{r}") for r in range(DEPTH)]
        xs_in = [sem(f"xs_in{r}") for r in range(DEPTH)]
        w_in = [sem(f"w_in{r}") for r in range(DEPTH)]
        xsT_done, xsT_ready = sem("xsT_done"), sem("xsT_ready")
        up_done, silu_ready, hid_ready = sem("up_done"), sem("silu_ready"), sem("hid_ready")
        hidT_done, hidT_ready = sem("hidT_done"), sem("hidT_ready")
        y_done, y_ready = sem("y_done"), sem("y_ready")
        y_out = [sem(f"y_out{r}") for r in range(DEPTH)]
        slots_now, slots_taken = sem("slots_now"), sem("slots_taken")
        y_got = [sem(f"y_got{r}") for r in range(2 * DEPTH)]
        sh_done, silu3_ready, hT3_ready = sem("sh_done"), sem("silu3_ready"), sem("hT3_ready")
        sh2_done, comb, ysel_free = sem("sh2_done"), sem("comb"), sem("ysel_free")
        stored = [sem(f"stored{b}") for b in range(2)]

        LN_STEPS, RSTD_STEPS = 2, 2
        PICK_STEPS, PICKED = 9, 6
        RANK_STEPS = 5
        COMB_STEPS = 3 * DEPTH
        CREDIT = 1
        N_POOL_SETUP, N_DVE_SETUP, N_WEIGHTS, N_ZERO = 14, 15, 5, SLOTS * D // (P * 1024)

        def place(i, u, k):
            s = DEPTH * HEAD_ROUNDS + u - k
            return DEPTH * i + s, i + s // DEPTH, s % DEPTH

        def live(t):
            return not isinstance(t, int) or 0 <= t < TILES

        def past(t, lag):
            return not isinstance(t, int) or t >= lag

        def rounds(eng, step):
            for i in range(-HEAD_ROUNDS, 0):
                for u in range(DEPTH):
                    step(i, u)
            with eng.Fori(0, LOOPS) as i:
                for u in range(DEPTH):
                    step(i, u)
            for i in range(LOOPS, LOOPS + TAIL_ROUNDS):
                for u in range(DEPTH):
                    step(i, u)

        def tile_cols(t, n=P):
            return bass.ds(t * n, n)

        def pair_rounds(eng, step, depth):
            for u in range(DEPTH):
                step(0, u)
            with eng.Fori(1, EPAIRS // DEPTH) as i:
                for u in range(DEPTH):
                    step(i, u)
            for u in range(depth - 1):
                step(EPAIRS // DEPTH, u)

        def pair_place(i, u, k):
            return DEPTH * i + (u - k), i + (u - k) // DEPTH, (u - k) % DEPTH

        def pair_live(j):
            return not isinstance(j, int) or 0 <= j < EPAIRS

        block = ctx.enter_context(nc.Block())

        @block.sync
        def _(sp):
            for n, w in enumerate((Wq, Wk, Wv, Wo)):
                sp.dma_start(raw[:, n, :], w).then_inc(weights_in, 16)
            sp.dma_start(raw_gate[:, :], gate_w).then_inc(weights_in, 16)
            sp.dma_start(ids_i[:, :], x.rearrange("b (n p) -> (b n) p", p=P)).then_inc(ids_in, 16)
            sp.wait_ge(consts_ready, 1)
            rows = P * 1024 // D
            for n in range(N_ZERO):
                sp.dma_start(xslots[n * rows:(n + 1) * rows, :].rearrange("(p a) d -> p (a d)", p=P),
                             zeros[:, :]).then_inc(zeroed, 16)
            sp.dma_start(yslots[SLOTS:SLOTS + 1, :], zeros[0:1, 0:D]).then_inc(zeroed, 16)
            sp.dma_start(shared13[:, 0, :], sw1).then_inc(shared_in, 16)
            sp.dma_start(shared13[:, 1, :], sw3).then_inc(shared_in, 16)
            sp.dma_start(shared2[:, :], sw2).then_inc(shared_in, 16)

            def load_weights(j, r):
                sp.dma_start(w13[:, r, :, 0, :], w1[bass.ds(j * 2, 2)].rearrange("e d h -> d e h")).then_inc(w_in[r], 16)
                sp.dma_start(w13[:, r, :, 1, :], w3[bass.ds(j * 2, 2)].rearrange("e d h -> d e h")).then_inc(w_in[r], 16)
                sp.dma_start(w2s[:, r, :], w2[bass.ds(j * 2, 2)].rearrange("e h d -> (e h) d")).then_inc(w_in[r], 16)

            def load_slots(j, r):
                sp.dma_start(xs[:, r, :].rearrange("p (e f) -> p e f", e=2),
                             xslots[bass.ds(j * (2 * CAP), 2 * CAP), :].rearrange("(e p i) d -> p e (i d)", e=2, i=2)
                             ).then_inc(xs_in[r], 16)

            for r in range(DEPTH):
                load_weights(r, r)

            def step(i, u):
                t, q, r = place(i, u, NORM1)
                if live(t):
                    sp.wait_ge(gathered[r], 16 * (q + 1))
                    sp.dma_start(hres[:, tile_cols(t)], hg[:, r, :]).then_inc(res_saved[r], 16)
                t, q, r = place(i, u, GATE)
                if live(t):
                    sp.wait_ge(mix_ready, t + 3)
                    sp.dma_start(x2T_all[:, tile_cols(t)], mixT[:, r % 2, 1, :]).then_inc(x2T_saved[r % 2], 16)

            rounds(sp, step)
            for r in range(DEPTH):
                sp.wait_ge(scattered[r], 32 * (TILES // DEPTH))
            for r in range(DEPTH):
                load_slots(r, r)

            def store_y(j, r):
                sp.wait_ge(y_ready, 2 * (j + 1))
                sp.dma_start(yslots[bass.ds(j * (2 * CAP), 2 * CAP), :].rearrange("(e p i) d -> p e (i d)", e=2, i=2),
                             ys[:, r, :].rearrange("p (e f) -> p e f", e=2)).then_inc(y_out[r], 16)

            def refill(j, r):
                if not isinstance(j, int) or j + DEPTH < EPAIRS:
                    sp.wait_ge(xsT_done, j + 1)
                    load_slots(j + DEPTH, r)
                if not isinstance(j, int) or 2 <= j < EPAIRS - 2:
                    sp.wait_ge(y_done, j - 1)
                    load_weights(j + 2, (r + 2) % DEPTH)
                if not isinstance(j, int) or j >= 3:
                    store_y(j - 3, (r - 3) % DEPTH)

            for r in range(DEPTH):
                refill(r, r)
            with sp.Fori(1, EPAIRS // DEPTH - 1) as i:
                for r in range(DEPTH):
                    refill(DEPTH * i + r, r)
            for r in range(DEPTH):
                refill(EPAIRS - DEPTH + r, r)
            for j in range(EPAIRS - 3, EPAIRS):
                store_y(j, j % DEPTH)

            with sp.Fori(0, TILES // (2 * DEPTH)) as g:
                for b in range(2):
                    sp.wait_ge(comb, CREDIT + COMB_STEPS * (2 * g + b + 1))
                    sp.dma_start(out_rows[bass.ds((2 * g + b) * (DEPTH * P), DEPTH * P), :].rearrange("(n p) d -> p n d", p=P),
                                 acc[b].rearrange("p (n d) -> p n d", d=D)).then_inc(stored[b], 16)
            for b in range(2):
                sp.wait_ge(stored[b], CREDIT + 16 * (TILES // (2 * DEPTH)))
            sp.wait_ge(zeroed, 16 * (N_ZERO + 1))

        @block.gpsimd
        def _(pool):
            done = [0]

            def link(ins):
                done[0] += 1
                ins.then_inc(pool_setup, 1)
                pool.wait_ge(pool_setup, done[0])

            pool.memset(zeros[:, :], 0.0).then_inc(consts_ready, 1)
            link(pool.memset(ident[:, :], 0.0))
            link(pool.affine_select(out=ident[:, :], in_=ident[:, :], compare_op=ALU.not_equal, fill=1.0, base=0,
                                    pattern=[[-1, P]], channel_multiplier=1))
            link(pool.memset(onesb[:, :], 1.0))
            link(pool.affine_select(out=before[:, :], in_=onesb[:, :], compare_op=ALU.is_ge, fill=0.0, base=-1,
                                    pattern=[[1, P]], channel_multiplier=-1))
            link(pool.memset(masks[:, :], 0.0))
            for half in range(2):
                rows = slice(half * W, half * W + W)
                for c in (P, 2 * P):
                    pool.affine_select(out=masks[rows, c:c + W], in_=masks[rows, c:c + W], compare_op=ALU.is_ge,
                                       fill=NEG, base=-1, pattern=[[1, W]], channel_multiplier=-1)
                for c in (W, P + W, 2 * P + W):
                    mask_ins = pool.affine_select(out=masks[rows, c:c + W], in_=masks[rows, c:c + W], compare_op=ALU.is_ge,
                                                  fill=NEG, base=0, pattern=[[-1, W]], channel_multiplier=1)
                link(mask_ins)
            link(pool.memset(masks[:, 0:W], NEG))
            link(pool.iota(expert_noi[:, :], pattern=[[1, E]], base=0, channel_multiplier=0))
            link(pool.memset(neghalf[:, :], -0.5))
            link(pool.memset(epscol[:, :], EPS))
            link(pool.memset(zero_i[:, :], 0))
            link(pool.memset(count[:, :], 0.0))
            link(pool.memset(xnT[:, :], 0.0))
            assert done[0] == N_POOL_SETUP

            def step(i, u):
                t, q, r = place(i, u, GATHER)
                if live(t):
                    pool.wait_ge(id_picked, t + 1)
                    if past(t, DEPTH):
                        pool.wait_ge(xn_ready, t - DEPTH + 1)
                        pool.wait_ge(res_saved[r], 16 * q)
                t, q, r = place(i, u, SCATTER)
                if live(t):
                    pool.wait_ge(ranking, RANK_STEPS * (t + 1))
                    if isinstance(t, int) and t == 0:
                        pool.wait_ge(zeroed, 16 * (N_ZERO + 1))
                a, _, ar = place(i, u, NORM1)
                b, _, _ = place(i, u, NORM2)
                n = RSTD_STEPS * a
                if live(a) or live(b):
                    lo, hi = (0 if live(a) else 1), (2 if live(b) else 1)
                    if live(a):
                        pool.wait_ge(ln1, LN_STEPS * (a + 1))
                    if live(b):
                        pool.wait_ge(ln2, LN_STEPS * (b + 1))
                    pool.tensor_tensor(rs[:, ar % 2, 0, lo:hi], mv[:, ar % 2, lo:hi, 1], epscol[:, lo:hi],
                                       ALU.add).then_inc(rstd, 1)
                    pool.wait_ge(rstd, n + 1)
                    pool.tensor_tensor(rs[:, ar % 2, 1, lo:hi], rs[:, ar % 2, 0, lo:hi], neghalf[:, lo:hi],
                                       ALU.pow).then_inc(rstd, 1)
                t, q, r = place(i, u, SCATTER)
                if live(t):
                    pool.wait_ge(rank_done, t + 1)
                    pool.tensor_tensor(count[:, :], count[:, :], pick[:, r % 2, 0, :], ALU.add).then_inc(counted, 1)
                    pool.wait_ge(counted, 2 * t + 1)
                    pool.tensor_tensor(count[:, :], count[:, :], pick[:, r % 2, 1, :], ALU.add).then_inc(counted, 1)
                t, q, r = place(i, u, GATHER)
                if live(t):
                    pool.indirect_dma_start(out=hg[:, r, :], out_offset=None, in_=tok_w[:, :],
                                            in_offset=bass.IndirectOffsetOnAxis(ap=row_id[:, r:r + 1], axis=0)
                                            ).then_inc(gathered[r], 16)
                t, q, r = place(i, u, SCATTER)
                if live(t):
                    for k in range(2):
                        pool.indirect_dma_start(out=xslots[:, :],
                                                out_offset=bass.IndirectOffsetOnAxis(ap=slot[:, r, k:k + 1], axis=0),
                                                in_=x2[:, r, :], in_offset=None, bounds_check=SLOTS - 1,
                                                oob_is_err=False).then_inc(scattered[r], 16)

            rounds(pool, step)

            for r in range(DEPTH):
                pool.wait_ge(y_out[r], CREDIT + 16 * (EPAIRS // DEPTH))
            with pool.Fori(0, TILES // (2 * DEPTH)) as g:
                for b in range(2):
                    pool.wait_ge(slots_now, 2 * g + b + 1)
                    pool.wait_ge(ysel_free, CREDIT + 2 * g + b)
                    pool.tensor_tensor(slot_now[:, b, :], slot_next[:, b, :], zero_i[:, :], ALU.add).then_inc(slots_taken, 1)
                    pool.wait_ge(slots_taken, 2 * g + b + 1)
                    pool.tensor_tensor(gate_scratch[:, :], neghalf[:, 0:1], epscol[:, 0:1], ALU.add)
                    for n in range(DEPTH):
                        m = b * DEPTH + n
                        for k in range(2):
                            pool.indirect_dma_start(
                                out=ysel[:, m, k, :], out_offset=None, in_=yslots[:, :],
                                in_offset=bass.IndirectOffsetOnAxis(ap=slot_now[:, b, 2 * n + k:2 * n + k + 1], axis=0)
                            ).then_inc(y_got[m], 16)

        @block.tensor
        def _(pe):
            pe.wait_ge(pool_setup, N_POOL_SETUP)
            pe.wait_ge(weights_in, 16 * N_WEIGHTS)
            for n in range(3):
                pe.transpose(ps[:, 0, n * P:(n + 1) * P], raw[:, n, :], ident[:, :])
            pe.transpose(ps[:, 2, 0:E], raw_gate[:, :], ident[0:E, 0:E]).then_inc(setup_T, 1)
            pe.wait_ge(dve_setup, 2)
            pe.transpose(ps[:, 1, 0:P], wo_perm[:, :], ident[:, :])
            pe.transpose(ps[:, 3, 0:TILES], ids_f[:, :], ident[0:TILES, 0:TILES]).then_inc(setup_T, 1)
            pe.wait_ge(dve_setup, N_DVE_SETUP)

            def score(i, u, pairs):
                t, q, r = place(i, u, SCORE)
                if not live(t):
                    return
                pe.wait_ge(qk_ready, t + 1)
                if past(t, 1):
                    pe.wait_ge(p_ready, PAIRS * (t - 1) + pairs[-1] + 1)
                c = P
                if r == 0:
                    start = (t % SEQ_TILES == 0) if isinstance(t, int) else (i & 1)
                    c = P - start * P
                for pair in pairs:
                    pe.matmul(S(pair), identb[:, :], masks[:, bass.ds(c, 2 * P)], start=True, stop=False)
                for blk in range(2):
                    for pair in pairs:
                        rows = slice(32 * pair, 32 * pair + 32)
                        c0 = (r % 2) * P + blk * W
                        mm = pe.matmul(S(pair)[:, blk * P:(blk + 1) * P],
                                       QT[rows, r % 2, blk, :, :].rearrange("p a q -> p (a q)"), KT[rows, c0:c0 + P],
                                       start=False, stop=(blk == 1))
                        if blk == 1:
                            mm.then_inc(s_done, 1)

            def turn_probs(t, r, blk):
                for pair in range(PAIRS):
                    mm = pe.transpose(PT(blk)[:, pair * P:(pair + 1) * P],
                                      prob[:, r % 2, blk, pair * P:(pair + 1) * P], ident[:, :])
                mm.then_inc(pT_done, 1)

            def step(i, u):
                c, _, cr = place(i, u, PROJ)
                e, _, er = place(i, u, VALUE)
                f, _, fr = place(i, u, OUTP)
                g, _, gr = place(i, u, GATE)
                h, _, hr = place(i, u, ROUTE)

                if live(c - 1):
                    pe.wait_ge(qk_ready, c)
                if live(g - 1):
                    pe.wait_ge(elog_ready, g)
                if live(f):
                    pe.wait_ge(attn_ready, 2 * (f + 1))
                    for blk in range(2):
                        mm = pe.matmul(p_fold[:, blk * W:(blk + 1) * W], attn[:, fr % 2, blk, :], fold2[:, :],
                                       start=True, stop=True)
                    mm.then_inc(fold_done, 1)
                if live(c):
                    pe.wait_ge(xn_ready, c + 1)
                    pe.transpose(p_xT, xn[:, cr % 2, :], ident[:, :]).then_inc(xT_done, 1)
                if live(g):
                    pe.wait_ge(x2_ready, g + 1)
                    pe.transpose(p_x2T, x2[:, gr, :], ident[:, :]).then_inc(x2T_done, 1)

                if live(e):
                    pe.wait_ge(p_ready, PAIRS * (e + 1))
                    if past(e, 1):
                        pe.wait_ge(pT_ready, 2 * e - 1)
                    if live(c - 1):
                        pe.wait_ge(v_ready, c)
                    turn_probs(e, er, 0)
                score(i, u, (0, 1))
                if live(e):
                    if past(e, 1):
                        pe.wait_ge(pT_ready, 2 * e)
                    turn_probs(e, er, 1)

                if live(c):
                    pe.wait_ge(xT_ready, c + 1)
                if live(f) or live(g):
                    pe.wait_ge(mix_ready, f + 1)
                if live(c):
                    cur = xnT[:, W + (cr % 2) * P:W + (cr % 2) * P + P]
                    pe.matmul(p_q, WqT[:, :], cur, start=True, stop=True)
                    pe.matmul(p_k, WkT[:, :], cur, start=True, stop=True).then_inc(qk_done, 1)
                if live(g):
                    pe.matmul(p_log, mixT[:, gr % 2, 1, :], gateT[:, :], start=True, stop=True).then_inc(log_done, 1)

                if live(e - 1):
                    pe.wait_ge(attn_ready, 2 * e)
                if live(f - 1):
                    pe.wait_ge(res_ready, f)
                if live(h - 1):
                    pe.wait_ge(rank_read, h)
                if live(f):
                    pe.matmul(p_wo, mixT[:, fr % 2, 0, :], WoT[:, :], start=True, stop=True).then_inc(wo_done, 1)
                if live(h):
                    pe.wait_ge(picking, PICK_STEPS * h + PICKED)
                    if past(h, 1):
                        pe.wait_ge(counted, 2 * h)
                    pe.matmul(p_rank, onesb[:, :], count[:, :], start=True, stop=False)
                    pe.matmul(p_rank, before[:, :], pick[:, hr % 2, 0, :], start=False, stop=False)
                    pe.matmul(p_rank, before[:, :], pick[:, hr % 2, 1, :], start=False, stop=True).then_inc(rank_done, 1)

                if live(c):
                    if live(e):
                        pe.wait_ge(pT_ready, 2 * e + 1)
                    if past(c, 1):
                        pe.wait_ge(v_ready, c)
                    for blk in range(2):
                        c0 = (cr % 2) * P + blk * W
                        mm = pe.matmul(p_v[:, blk * P:(blk + 1) * P], xnT[:, c0:c0 + P], WvT[:, :], start=True, stop=True)
                    mm.then_inc(v_done, 1)

                score(i, u, (2, 3))

                if live(e):
                    if live(f):
                        pe.wait_ge(res_ready, f + 1)
                    if live(h):
                        pe.wait_ge(rank_read, h + 1)
                    pe.wait_ge(v_ready, e + 1)
                    for blk in range(2):
                        pe.wait_ge(pT_ready, 2 * e + blk + 1)
                        for pair in range(PAIRS):
                            o0 = (blk * PAIRS + pair) * VW
                            mm = pe.matmul(p_o[:, o0:o0 + VW], probT[:, blk, pair * P:(pair + 1) * P],
                                           V[:, er, blk, pair * VW:(pair + 1) * VW], start=True, stop=True)
                        mm.then_inc(o_done, 1)

            rounds(pe, step)

            pe.wait_ge(attn_ready, 2 * TILES)

            def pair_step(i, u):
                j, q, r = pair_place(i, u, 0)
                if pair_live(j):
                    pe.wait_ge(xs_in[r], 16 * (q + 1))
                    if past(j, 2):
                        pe.wait_ge(xsT_ready, j - 1)
                    for s in range(4):
                        mm = pe.transpose(ps[:, r % 2, s * P:(s + 1) * P], xs[:, r, s * P:(s + 1) * P], ident[:, :])
                    mm.then_inc(xsT_done, 1)
                j, q, r = pair_place(i, u, 1)
                if pair_live(j):
                    pe.wait_ge(w_in[r], 48 * (q + 1))
                    pe.wait_ge(xsT_ready, j + 1)
                    if past(j, 2):
                        pe.wait_ge(hid_ready, j - 1)
                    for s in range(4):
                        mm = pe.matmul(ps[:, 2 + r % 2, s * P:(s + 1) * P], xsT[:, r % 2, s * P:(s + 1) * P],
                                       w13[:, r, s // 2, :, :], start=True, stop=True)
                    mm.then_inc(up_done, 1)
                j, q, r = pair_place(i, u, 2)
                if pair_live(j):
                    pe.wait_ge(hid_ready, j + 1)
                    if past(j, 1):
                        pe.wait_ge(hidT_ready, j)
                    for n in range(2):
                        mm = pe.transpose(ps[:, 4, n * P:(n + 1) * P],
                                          hid[:, r % 2, n, :, :].rearrange("p e h -> p (e h)"), ident[:, :])
                    mm.then_inc(hidT_done, 1)
                j, q, r = pair_place(i, u, 3)
                if pair_live(j):
                    pe.wait_ge(hidT_ready, j + 1)
                    if past(j, 1):
                        pe.wait_ge(y_ready, 2 * j)
                    for n in range(2):
                        for e in range(2):
                            rows = slice(e * H, (e + 1) * H)
                            c = (r % 2) * 2 * P + n * P
                            mm = pe.matmul(ps[:, 5 + e, c:c + P], hidT[rows, r % 2, n * P:(n + 1) * P],
                                           w2s[rows, r, :], start=True, stop=True)
                    mm.then_inc(y_done, 1)

            pair_rounds(pe, pair_step, 4)

            pe.wait_ge(shared_in, 48)
            for b in range(2):
                pe.wait_ge(x2T_saved[b], 16 * (TILES // 2))
            pe.wait_ge(y_ready, 2 * EPAIRS)
            with pe.Fori(0, TILES // (2 * DEPTH)) as g:
                for b in range(2):
                    pe.wait_ge(hT3_ready, CREDIT + 2 * g + b)
                    cols = bass.ds((2 * g + b) * (DEPTH * P), DEPTH * P)
                    for n in range(2):
                        mm = pe.matmul(ps[:, n, :], shared13[:, n, :], x2T_all[:, cols], start=True, stop=True)
                    mm.then_inc(sh_done, 1)
                    pe.wait_ge(hT3_ready, CREDIT + 2 * g + b + 1)
                    pe.wait_ge(comb, CREDIT + COMB_STEPS * (2 * g + b))
                    for n in range(DEPTH):
                        mm = pe.matmul(ps[:, 2, n * P:(n + 1) * P], hT3[b][:, n * P:(n + 1) * P], shared2[:, :],
                                       start=True, stop=True)
                    mm.then_inc(sh2_done, 1)

        @block.vector
        def _(dve):
            done = [0]

            def link(ins):
                done[0] += 1
                ins.then_inc(dve_setup, 1)
                dve.wait_ge(dve_setup, done[0])

            dve.wait_ge(weights_in, 16 * N_WEIGHTS)
            dve.wait_ge(ids_in, 16)
            link(dve.tensor_copy(wo_perm[:, :].rearrange("o (a b d) -> o a b d", a=2, b=PAIRS),
                                 raw[:, 3, :].rearrange("o (b a d) -> o a b d", a=2, b=PAIRS)))
            link(dve.tensor_copy(ids_f[:, :], ids_i[:, :]))
            dve.wait_ge(setup_T, 1)
            for n, wT in enumerate((WqT, WkT, WvT)):
                link(dve.tensor_copy(wT[:, :], ps[:, 0, n * P:(n + 1) * P]))
            link(dve.tensor_copy(gateT[:, :], ps[:, 2, 0:E]))
            dve.wait_ge(setup_T, 2)
            dve.tensor_copy(idsT[:, :], ps[:, 3, 0:TILES])
            link(dve.tensor_copy(WoT[:, :], ps[:, 1, 0:P]))
            dve.wait_ge(pool_setup, N_POOL_SETUP)
            dve.tensor_copy(expert_no[:, :], expert_noi[:, :])
            link(dve.tensor_copy(identb[:, :], ident[:, :]))
            link(dve.tensor_tensor(fold2[:, :], ident[:, 0:W], ident[:, W:2 * W], ALU.add))
            view = ident[:, :].rearrange("p (g c) -> p g c", c=2 * HD)
            for a in range(2):
                link(dve.tensor_reduce(rowmask[:, a:a + 1], view[:, :, a * HD:(a + 1) * HD], AX.XY, ALU.add))
            link(dve.memset(attn[:, :, :, :], 0.0))
            link(dve.memset(V[:, :, :, :], 1.0))
            link(dve.memset(KT[:, :], 0.0))
            link(dve.memset(idx[:, :, :], 0.0))
            assert done[0] == N_DVE_SETUP

            def row_max(i, u, pair):
                t, q, r = place(i, u, SCORE)
                if live(t):
                    n = PAIRS * t + pair
                    dve.wait_ge(s_done, n + 1)
                    dve.tensor_reduce(mx[:, r % 2, pair, :], S(pair).rearrange("p (b k) -> p b k", b=2), AX.X,
                                      ALU.max).then_inc(max_done, 1)
                    dve.wait_ge(max_done, n + 1)
                    if past(t, 2):
                        dve.wait_ge(p_ready, n - 2 * PAIRS + 1)
                    dve.tensor_scalar(nmx[:, r % 2, pair, :], mx[:, r % 2, pair, :], -SCALE, None,
                                      ALU.mult).then_inc(max_ready, 1)

            def step(i, u):
                gt, gq, gr = place(i, u, GATHER)
                at, aq, ar = place(i, u, NORM1)
                bt, bq, br = place(i, u, NORM2)
                t, q, r = place(i, u, ROUTE)
                n, b = PICK_STEPS * t, r % 2
                ab = ar % 2
                if live(at):
                    dve.wait_ge(gathered[ar], 16 * (aq + 1))
                if live(bt):
                    dve.wait_ge(res_ready, bt + 1)
                if live(t):
                    dve.wait_ge(elog_ready, t + 1)
                    dve.tensor_scalar(negd[:, :], elog[:, b, :], -1.0, -1.0, ALU.mult, ALU.add).then_inc(picking, 1)
                if live(at):
                    dve.bn_stats(st1[:, :], hg[:, ar, :]).then_inc(ln1, 1)
                if live(bt):
                    dve.bn_stats(st2[:, :], hres[:, tile_cols(bt)]).then_inc(ln2, 1)
                    dve.wait_ge(ln2, LN_STEPS * bt + 1)
                if live(at):
                    dve.wait_ge(ln1, LN_STEPS * at + 1)
                if live(t):
                    dve.wait_ge(picking, n + 1)
                if live(gt):
                    if past(gt, DEPTH):
                        dve.wait_ge(gathered[gr], 16 * gq)
                    dve.tensor_copy(row_id[:, gr:gr + 1], idsT[:, bass.ds(gt, 1)]).then_inc(id_picked, 1)
                if live(at):
                    dve.bn_aggr(mv[:, ab, 0, :], st1[:, :]).then_inc(ln1, 1)
                if live(bt):
                    dve.bn_aggr(mv[:, ab, 1, :], st2[:, :]).then_inc(ln2, 1)
                if live(t):
                    dve.max(top[:, :], negd[:, :]).then_inc(picking, 1)
                    dve.wait_ge(picking, n + 2)
                    dve.reciprocal(negs[:, :], top[:, 0:2]).then_inc(picking, 1)
                    dve.max_index(topi[:, :], top[:, :], negd[:, :]).then_inc(picking, 1)
                    dve.wait_ge(picking, n + 4)
                    dve.tensor_copy(idx[:, b, :], topi[:, 0:2]).then_inc(picking, 1)
                    dve.wait_ge(picking, n + 5)
                    if past(t, 2):
                        dve.wait_ge(counted, 2 * (t - 1))
                    dve.tensor_tensor(pick[:, b, :, :], expert_no[:, :].unsqueeze(1).to_broadcast([P, 2, E]),
                                      idx[:, b, :].unsqueeze(2).to_broadcast([P, 2, E]), ALU.is_equal).then_inc(picking, 1)
                row_max(i, u, 0)
                row_max(i, u, 1)
                t, q, r = place(i, u, NORM1)
                if live(t):
                    dve.wait_ge(rstd, RSTD_STEPS * (t + 1))
                    if past(t, 2):
                        dve.wait_ge(xT_done, t - 1)
                    dve.tensor_scalar(xn[:, r % 2, :], hg[:, r, :], mv[:, r % 2, 0, 0:1], rs[:, r % 2, 1, 0:1], ALU.subtract,
                                      ALU.mult).then_inc(xn_ready, 1)
                t, q, r = place(i, u, NORM2)
                if live(t):
                    dve.wait_ge(rstd, RSTD_STEPS * (t + NORM2 - NORM1 + 1))
                    if past(t, DEPTH):
                        dve.wait_ge(x2T_done, t - DEPTH + 1)
                        dve.wait_ge(scattered[r], 32 * q)
                    dve.tensor_scalar(x2[:, r, :], hres[:, tile_cols(t)], mv[:, r % 2, 1, 0:1], rs[:, r % 2, 1, 1:2], ALU.subtract,
                                      ALU.mult).then_inc(x2_ready, 1)
                t, q, r = place(i, u, ROUTE)
                if live(t):
                    n = PICK_STEPS * t
                    dve.tensor_scalar(tsum[:, :], negs[:, 0:1], negs[:, 1:2], -1e-20, ALU.add, ALU.add).then_inc(picking, 1)
                    dve.wait_ge(picking, n + 7)
                    dve.reciprocal(trec[:, :], tsum[:, :]).then_inc(picking, 1)
                    dve.wait_ge(picking, n + 8)
                    dve.tensor_scalar(gain_all[:, tile_cols(t, 2)], negs[:, :], trec[:, 0:1], ROUTE_SCALE, ALU.mult,
                                      ALU.mult).then_inc(picking, 1)
                h, _, hr = place(i, u, ROUTE)
                t, q, r = place(i, u, OUTP)
                if live(h):
                    dve.wait_ge(rank_done, h + 1)
                if live(t):
                    dve.wait_ge(wo_done, t + 1)
                    dve.wait_ge(res_saved[r], 16 * (q + 1))
                    dve.tensor_tensor(hres[:, tile_cols(t)], p_wo, hres[:, tile_cols(t)], ALU.add).then_inc(res_ready, 1)
                if live(h):
                    dve.tensor_tensor(rank[:, :, :], p_rank.unsqueeze(1).to_broadcast([P, 2, E]), pick[:, hr % 2, :, :],
                                      ALU.mult).then_inc(rank_read, 1)
                row_max(i, u, 2)
                row_max(i, u, 3)
                t, q, r = place(i, u, VALUE)
                if live(t):
                    dve.wait_ge(o_done, 2 * (t + 1))
                    o = p_o.rearrange("p (b g c) -> p b g c", b=2, c=VW)
                    rr = rsum[:, r % 2, :].rearrange("p (b g) -> p b g", b=2)
                    dve.reciprocal(rr, o[:, :, :, 2 * HD]).then_inc(rsum_ready, 1)
                    dve.wait_ge(rsum_ready, t + 1)
                    if past(t, 2):
                        dve.wait_ge(fold_done, t - 1)
                    for a in range(2):
                        rows = slice(a * W, (a + 1) * W)
                        dve.tensor_tensor(
                            attn[rows, r % 2, :, a * W:(a + 1) * W].rearrange("p b (g d) -> p b g d", d=HD),
                            o[rows, :, :, a * HD:(a + 1) * HD],
                            rr[rows].unsqueeze(3).to_broadcast([W, 2, PAIRS, HD]), ALU.mult).then_inc(attn_ready, 1)
                t, q, r = place(i, u, ROUTE)
                if live(t):
                    n = RANK_STEPS * t
                    b = r % 2
                    dve.wait_ge(rank_read, t + 1)
                    dve.tensor_reduce(pos[:, :], rank[:, :, :], AX.X, ALU.add).then_inc(ranking, 1)
                    dve.wait_ge(ranking, n + 1)
                    dve.tensor_scalar(over[:, :], pos[:, :], float(CAP), float(2 * SLOTS), ALU.is_ge, ALU.mult)
                    dve.scalar_tensor_tensor(slotf[:, :], idx[:, b, :], float(CAP), pos[:, :], ALU.mult,
                                             ALU.add).then_inc(ranking, 1)
                    dve.wait_ge(ranking, n + 2)
                    dve.tensor_tensor(slotf[:, :], slotf[:, :], over[:, :], ALU.add).then_inc(ranking, 1)
                    dve.wait_ge(ranking, n + 3)
                    dve.tensor_scalar(slot_all[:, tile_cols(t, 2)], slotf[:, :], float(SLOTS), None,
                                      ALU.min).then_inc(ranking, 1)
                    dve.tensor_copy(slot[:, r, :], slotf[:, :]).then_inc(ranking, 1)

            rounds(dve, step)

            for s in y_out:
                dve.engine_nop().then_inc(s, CREDIT)

            def pair_step(i, u):
                j, q, r = pair_place(i, u, 1)
                if pair_live(j):
                    b = r % 2
                    up = ps[:, 2 + b, :].rearrange("p (s a h) -> p s a h", s=4, a=2)
                    dve.wait_ge(silu_ready, j + 1)
                    if past(j, 2):
                        dve.wait_ge(hidT_done, j - 1)
                    dve.tensor_tensor(hid[:, b, :, :, :].rearrange("p n e h -> p e n h"),
                                      up[:, :, 1, :].rearrange("p (e n) h -> p e n h", e=2),
                                      silu[:, b, :, :].rearrange("p (e n) h -> p e n h", e=2),
                                      ALU.mult).then_inc(hid_ready, 1)
                j, q, r = pair_place(i, u, 3)
                if pair_live(j):
                    dve.wait_ge(y_done, j + 1)
                    if past(j, DEPTH):
                        dve.wait_ge(y_out[r], CREDIT + 16 * q)
                    dve.tensor_copy(ys[:, r, 0:2 * P], ps[:, 5, (r % 2) * 2 * P:(r % 2 + 1) * 2 * P]).then_inc(y_ready, 1)

            pair_rounds(dve, pair_step, 4)

            for b in range(2):
                dve.tensor_copy(slot_next[:, b, :], slot_all[:, b * 2 * DEPTH:(b + 1) * 2 * DEPTH]).then_inc(slots_now, 1)
            for s in (hT3_ready, comb, *stored):
                dve.engine_nop().then_inc(s, CREDIT)
            for b in range(2):
                dve.engine_nop().then_inc(ysel_free, 1)
            with dve.Fori(0, TILES // (2 * DEPTH)) as g:
                for b in range(2):
                    gg = 2 * g + b
                    dve.wait_ge(silu3_ready, gg + 1)
                    dve.tensor_tensor(hT3[b], ps[:, 1, :], silu3[b], ALU.mult).then_inc(hT3_ready, 1)
                    dve.wait_ge(sh2_done, gg + 1)
                    dve.wait_ge(stored[b], CREDIT + 16 * g)
                    for n in range(DEPTH):
                        m = b * DEPTH + n
                        a = acc[b][:, n * P:(n + 1) * P]
                        t = gg * DEPTH + n
                        c = COMB_STEPS * gg + 3 * n
                        dve.tensor_tensor(a, ps[:, 2, n * P:(n + 1) * P], hres[:, tile_cols(t)], ALU.add).then_inc(comb, 1)
                        dve.wait_ge(y_got[m], 32 * (g + 1))
                        for k in range(2):
                            dve.wait_ge(comb, CREDIT + c + k + 1)
                            ins = dve.scalar_tensor_tensor(a, ysel[:, m, k, :], gain_all[:, bass.ds(2 * t + k, 1)], a,
                                                           ALU.mult, ALU.add).then_inc(comb, 1)
                    dve.wait_ge(comb, CREDIT + COMB_STEPS * (gg + 1))
                    dve.wait_ge(slots_taken, gg + 1)
                    nxt = (gg + 2) & (TILES // DEPTH - 1)
                    dve.tensor_copy(slot_next[:, b, :], slot_all[:, bass.ds(nxt * (2 * DEPTH), 2 * DEPTH)]).then_inc(slots_now, 1)
                    dve.engine_nop().then_inc(ysel_free, 1)

        @block.scalar
        def _(act):
            act.wait_ge(dve_setup, N_DVE_SETUP)

            def exps(i, u, pair):
                t, q, r = place(i, u, SCORE)
                if live(t):
                    act.wait_ge(max_ready, PAIRS * t + pair + 1)
                    if past(t, 2) and pair == 0:
                        act.wait_ge(pT_done, 2 * (t - 1))
                    for blk in range(2):
                        ins = act.activation(prob[:, r % 2, blk, pair * P:(pair + 1) * P],
                                             S(pair)[:, blk * P:(blk + 1) * P], ACT.Exp,
                                             bias=nmx[:, r % 2, pair, blk:blk + 1], scale=SCALE)
                    ins.then_inc(p_ready, 1)

            def copy_pT(i, u, blk):
                t, q, r = place(i, u, VALUE)
                if live(t):
                    act.wait_ge(pT_done, 2 * t + blk + 1)
                    if past(t, 1):
                        act.wait_ge(o_done, 2 * t + blk - 1)
                    act.copy(probT[:, blk, :], PT(blk)).then_inc(pT_ready, 1)

            def step(i, u):
                c, _, cr = place(i, u, PROJ)
                f, _, fr = place(i, u, OUTP)
                g, gq, gr = place(i, u, GATE)
                if live(c):
                    act.wait_ge(xT_done, c + 1)
                    if past(c, 1):
                        act.wait_ge(v_done, c)
                        act.wait_ge(qk_done, c)
                if live(f):
                    act.wait_ge(fold_done, f + 1)
                    if past(f, 2):
                        act.wait_ge(wo_done, f - 1)
                if live(g):
                    act.wait_ge(x2T_done, g + 1)
                    if past(g, 2):
                        act.wait_ge(log_done, g - 1)
                        act.wait_ge(x2T_saved[gr % 2], 16 * (2 * gq + gr // 2))
                if live(c):
                    if cr % 2:
                        act.copy(xnT[:, 0:W], p_xT[:, W:P])
                    act.copy(xnT[:, W + (cr % 2) * P:W + (cr % 2 + 1) * P], p_xT).then_inc(xT_ready, 1)
                if live(f) or live(g):
                    lo, hi = (0 if live(f) else 1), (2 if live(g) else 1)
                    act.copy(mixT[:, fr % 2, lo:hi, :], p_mix.rearrange("p (n c) -> p n c", n=2)[:, lo:hi, :]
                             ).then_inc(mix_ready, 1)
                copy_pT(i, u, 0)
                exps(i, u, 0)
                exps(i, u, 1)
                copy_pT(i, u, 1)
                if live(g):
                    act.wait_ge(log_done, g + 1)
                    if past(g, 2):
                        act.wait_ge(picking, PICK_STEPS * (g - 1))
                if live(c):
                    act.wait_ge(qk_done, c + 1)
                    if past(c, 1):
                        act.wait_ge(s_done, PAIRS * c)
                    for a in range(2):
                        act.activation(QT[:, cr % 2, :, a, :], p_q.rearrange("p (b q) -> p b q", b=2), ACT.Identity,
                                       scale=rowmask[:, a:a + 1])
                    if cr % 2:
                        act.copy(KT[:, 0:W], p_k[:, W:P])
                    act.copy(KT[:, W + (cr % 2) * P:W + (cr % 2 + 1) * P], p_k).then_inc(qk_ready, 1)
                if live(g):
                    act.activation(elog[:, gr % 2, :], p_log, ACT.Exp, scale=-1.0).then_inc(elog_ready, 1)
                exps(i, u, 2)
                exps(i, u, 3)
                if live(c):
                    act.wait_ge(v_done, c + 1)
                    if past(c, DEPTH):
                        act.wait_ge(o_done, 2 * (c - DEPTH + 1))
                    act.copy(V[:, cr, :, :].rearrange("p b (g c) -> p b g c", c=VW)[:, :, :, 0:2 * HD],
                             p_v.rearrange("p (b g c) -> p b g c", b=2, c=2 * HD)).then_inc(v_ready, 1)

            rounds(act, step)

            def pair_step(i, u):
                j, q, r = pair_place(i, u, 0)
                if pair_live(j):
                    act.wait_ge(xsT_done, j + 1)
                    if past(j, 2):
                        act.wait_ge(up_done, j - 1)
                    act.copy(xsT[:, r % 2, :], ps[:, r % 2, :]).then_inc(xsT_ready, 1)
                j, q, r = pair_place(i, u, 1)
                if pair_live(j):
                    act.wait_ge(up_done, j + 1)
                    if past(j, 2):
                        act.wait_ge(hid_ready, j - 1)
                    act.activation(silu[:, r % 2, :, :],
                                   ps[:, 2 + r % 2, :].rearrange("p (s a h) -> p s a h", s=4, a=2)[:, :, 0, :],
                                   ACT.Silu).then_inc(silu_ready, 1)
                j, q, r = pair_place(i, u, 2)
                if pair_live(j):
                    act.wait_ge(hidT_done, j + 1)
                    if past(j, 2):
                        act.wait_ge(y_done, j - 1)
                    act.copy(hidT[:, r % 2, :], ps[:, 4, 0:2 * P]).then_inc(hidT_ready, 1)
                j, q, r = pair_place(i, u, 3)
                if pair_live(j):
                    act.wait_ge(y_done, j + 1)
                    if past(j, DEPTH):
                        act.wait_ge(y_out[r], CREDIT + 16 * q)
                    act.copy(ys[:, r, 2 * P:4 * P], ps[:, 6, (r % 2) * 2 * P:(r % 2 + 1) * 2 * P]).then_inc(y_ready, 1)

            pair_rounds(act, pair_step, 4)

            act.wait_ge(y_ready, 2 * EPAIRS)
            with act.Fori(0, TILES // (2 * DEPTH)) as g:
                for b in range(2):
                    act.wait_ge(sh_done, 2 * g + b + 1)
                    act.activation(silu3[b], ps[:, 0, :], ACT.Silu).then_inc(silu3_ready, 1)


_INS = ['x', 'L0_tok_w', 'L0_attn_Wq', 'L0_attn_Wk', 'L0_attn_Wv', 'L0_attn_Wo', 'L0_ffn_gate_w', 'L0_ffn_w1',
        'L0_ffn_w3', 'L0_ffn_w2', 'L0_ffn_sw1', 'L0_ffn_sw3', 'L0_ffn_sw2']
_OUTS = [((8, 1024, 128), 'float32')]


def kernel(**inputs):
    import numpy as _np
    import concourse.bacc as _bacc
    from concourse import mybir as _mybir
    from concourse.bass_utils import run_bass_kernel_spmd as _run

    nc = _bacc.Bacc("TRN2", target_bir_lowering=False, num_devices=1)
    arrays, args = {}, []
    for name in _INS:
        a = _np.ascontiguousarray(inputs[name])
        arrays[f"in_{name}_dram"] = a
        args.append(nc.dram_tensor(f"in_{name}_dram", a.shape, _mybir.dt.from_np(a.dtype), kind="ExternalInput").ap())
    for i, (shape, dtype) in enumerate(_OUTS):
        dt = _mybir.dt.from_np(_np.dtype(dtype))
        args.append(nc.dram_tensor(f"out_{i}_dram", shape, dt, kind="ExternalOutput").ap())
    lm_tower(nc, *args)
    r = _run(nc, [arrays], core_ids=[0])
    return r.results[0]["out_0_dram"]
```

```python
from contextlib import ExitStack

import concourse.bass as bass
from concourse import mybir

F32, BF16, I32, U32 = mybir.dt.float32, mybir.dt.bfloat16, mybir.dt.int32, mybir.dt.uint32
ALU = mybir.AluOpType
ACT = mybir.ActivationFunctionType
AX = mybir.AxisListType

P = 128
HEADS, HD = 8, 16
PAIRS = HEADS // 2
W = 64
EPS = 1e-5
SCALE = HD ** -0.5
MASKED = 1e30
CAP, ROUTE_SCALE = 256, 2.5
DEPTH = 4
HEAD_ROUNDS, TAIL_ROUNDS = 3, 3

GATHER, NORM1, PROJ, SCORE, VALUE, _, OUTP, NORM2, GATE, ROUTE, SCATTER = range(11)


def lm_tower(nc, x, tok_w, Wq, Wk, Wv, Wo, gate_w, w1, w3, w2, sw1, sw3, sw2, out):
    BATCH, SEQ = x.shape
    E, D, H = w1.shape
    TILES = BATCH * SEQ // P
    SEQ_TILES = SEQ // P
    LOOPS = TILES // DEPTH - HEAD_ROUNDS
    EPAIRS = E // 2
    SLOTS = E * CAP
    VW = 2 * HD + 1
    assert D == P and SEQ_TILES % 8 == 0 and 2 * H == P and E == W

    out_rows = out.rearrange("b s d -> (b s) d")
    xslots = nc.dram_tensor("xslots", [SLOTS, D], F32, kind="Internal").ap()
    yslots = nc.dram_tensor("yslots", [SLOTS + 1, D], F32, kind="Internal").ap()

    ctx = ExitStack()
    with ctx:
        def sb(name, shape, dt=F32):
            return ctx.enter_context(nc.sbuf_tensor(name, shape, dt))

        def sem(name):
            return ctx.enter_context(nc.semaphore(name))

        ident = sb("ident", [P, P])
        identb = sb("identb", [P, P], BF16)
        fold2 = sb("fold2", [P, W])
        before = sb("before", [P, P], BF16)
        base = sb("base", [P, E], BF16)
        count = sb("count", [P, E], BF16)
        onesb = sb("onesb", [P, P], BF16)
        masks = sb("masks", [P, 3 * P], BF16)
        qscale = sb("qscale", [P, 2])
        limit_of = sb("limit_of", [P, E])
        expert_noi = sb("expert_noi", [P, E], I32)
        neghalf = sb("neghalf", [P, 2])
        epscol = sb("epscol", [P, 2])
        zeros = sb("zeros", [P, 1024])
        raw = sb("raw", [P, 4, P])
        wo_perm = sb("wo_perm", [P, P])
        raw_gate = sb("raw_gate", [E, P])
        WqT, WkT, WvT, WoT = (sb(n, [P, P]) for n in ("WqT", "WkT", "WvT", "WoT"))
        gateT = sb("gateT", [P, E])
        shared13 = sb("shared13", [P, 2, P])
        shared2 = sb("shared2", [P, P])
        ids_i = sb("ids_i", [TILES, P], I32)
        ids_f = sb("ids_f", [TILES, P])
        idsT = sb("idsT", [P, TILES])

        hres = sb("hres", [P, TILES * P])
        x2T_all = sb("x2T_all", [P, TILES * P])
        slot_all = sb("slot_all", [P, 2 * TILES], I32)
        top_all = sb("top_all", [P, 2 * TILES])
        best_all = sb("best_all", [P, 2 * TILES])
        sum_all, inv_all = sb("sum_all", [P, TILES]), sb("inv_all", [P, TILES])
        gain_all = sb("gain_all", [P, 2 * TILES])

        row_id = sb("row_id", [P, DEPTH], I32)
        hg = sb("hg", [P, DEPTH, P])
        st1, st2 = sb("st1", [P, 6]), sb("st2", [P, 6])
        mv = sb("mv", [P, 2, 2, 2])
        rs = sb("rs", [P, 2, 2, 2])
        xn = sb("xn", [P, 2, P])
        xnT = sb("xnT", [P, W + 2 * P])
        KT = sb("KT", [P, W + DEPTH * P])
        QT = sb("QT", [P, 2, 2, 2, W])
        V = sb("V", [P, DEPTH, 2, PAIRS * VW])
        low = sb("low", [P, 2, PAIRS, 2])
        prob = sb("prob", [P, 2, 2, 2 * 2 * P])
        probT = sb("probT", [P, 2, 2 * 2 * P])
        rsum = sb("rsum", [P, 2, 2 * PAIRS])
        attn = sb("attn", [P, 2, 2, P])
        mixT = sb("mixT", [P, 2, 2, P])
        x2 = sb("x2", [P, DEPTH, P])
        elog = sb("elog", [P, 2, E])
        negd = sb("negd", [P, E])
        top = sb("top", [P, 8])
        topi = sb("topi", [P, 8], U32)
        limit = sb("limit", [P, 2])
        pick = sb("pick", [P, 2, 2, E], BF16)
        rank = sb("rank", [P, 2, E])
        seat, over = sb("seat", [P, 2]), sb("over", [P, 2])
        slot = sb("slot", [P, DEPTH, 2], I32)

        xs = sb("xs", [P, DEPTH, 4 * P])
        w13 = sb("w13", [P, DEPTH, 2, 2, H])
        w2s = sb("w2s", [P, DEPTH, P])
        xsT = sb("xsT", [P, 2, 4 * P])
        silu = sb("silu", [P, 2, 4, H])
        hid = sb("hid", [P, 2, 2, 2, H])
        hidT = sb("hidT", [P, 2, 2 * P])
        ys = sb("ys", [P, DEPTH, 4 * P])

        ysel = sb("ysel", [P, 2 * DEPTH, 2, P])
        slot_next = sb("slot_next", [P, 2, 2 * DEPTH], I32)
        slot_now = sb("slot_now", [P, 2, 2 * DEPTH], I32)
        zero_i = sb("zero_i", [P, 2 * DEPTH], I32)
        gate_scratch = sb("gate_scratch", [P, 1])
        silu3 = [xsT[:, 0, :], xsT[:, 1, :]]
        hT3 = [prob[:, 0, 0, :], prob[:, 0, 1, :]]
        acc = [prob[:, 1, 0, :], prob[:, 1, 1, :]]

        ps = ctx.enter_context(nc.psum_tensor("ps", [P, 8, 512], F32))

        def S(pair):
            return ps[:, pair, 0:2 * P]

        def PT(half):
            return ps[:, 4 + half, :]

        p_v = ps[:, 4, 0:2 * P]
        p_xT, p_mix = ps[:, 6, 0:P], ps[:, 6, P:3 * P]
        p_fold, p_x2T = ps[:, 6, P:2 * P], ps[:, 6, 2 * P:3 * P]
        p_q, p_k, p_log = ps[:, 6, 0:P], ps[:, 6, P:2 * P], ps[:, 6, 2 * P:2 * P + E]
        p_wo, p_rank = ps[:, 7, 0:P], ps[:, 7, P:P + E]
        p_o = ps[:, 7, 0:2 * PAIRS * VW]

        consts_ready = sem("consts_ready")
        pool_setup = sem("pool_setup")
        dve_setup = sem("dve_setup")
        weights_in = sem("weights_in")
        ids_in = sem("ids_in")
        shared_in = sem("shared_in")
        setup_T = sem("setup_T")
        zeroed = sem("zeroed")
        id_picked = sem("id_picked")
        gathered = [sem(f"gathered{r}") for r in range(DEPTH)]
        res_saved = [sem(f"res_saved{r}") for r in range(DEPTH)]
        stats1, stats2, aggr1, aggr2 = sem("stats1"), sem("stats2"), sem("aggr1"), sem("aggr2")
        var_ready, rstd, xn_ready = sem("var_ready"), sem("rstd"), sem("xn_ready")
        xT_done, xT_ready = sem("xT_done"), sem("xT_ready")
        qk_done, qk_ready = sem("qk_done"), sem("qk_ready")
        v_done, v_ready = sem("v_done"), sem("v_ready")
        s_done, low_ready, p_ready, pT_done, pT_ready = (
            [sem(f"{name}{half}") for half in range(2)] for name in ("s_done", "low_ready", "p_ready", "pT_done", "pT_ready"))
        o_done, rsum_ready, attn_ready = sem("o_done"), sem("rsum_ready"), sem("attn_ready")
        fold_done, mix_ready = sem("fold_done"), sem("mix_ready")
        wo_done, res_ready = sem("wo_done"), sem("res_ready")
        x2_ready = sem("x2_ready")
        x2T_done, counted_first, counted = sem("x2T_done"), sem("counted_first"), sem("counted")
        x2T_saved = [sem(f"x2T_saved{b}") for b in range(2)]
        log_done, elog_ready = sem("log_done"), sem("elog_ready")
        negd_ready, top_ready, top_saved = sem("negd_ready"), sem("top_ready"), sem("top_saved")
        topi_ready, limit_ready, pick_ready = sem("topi_ready"), sem("limit_ready"), sem("pick_ready")
        rank_done, rank_read, seat_ready = sem("rank_done"), sem("rank_read"), sem("seat_ready")
        over_ready, slot_ready, slots_saved, gains = sem("over_ready"), sem("slot_ready"), sem("slots_saved"), sem("gains")
        scattered = [sem(f"scattered{r}") for r in range(DEPTH)]
        xs_in = [sem(f"xs_in{r}") for r in range(DEPTH)]
        w_in = [sem(f"w_in{r}") for r in range(DEPTH)]
        xsT_done, xsT_ready = sem("xsT_done"), sem("xsT_ready")
        up_done, silu_ready, hid_ready = sem("up_done"), sem("silu_ready"), sem("hid_ready")
        hidT_done, hidT_ready = sem("hidT_done"), sem("hidT_ready")
        y_done, y_ready = sem("y_done"), sem("y_ready")
        y_out = [sem(f"y_out{r}") for r in range(DEPTH)]
        slots_now, slots_taken = sem("slots_now"), sem("slots_taken")
        y_got = [sem(f"y_got{r}") for r in range(2 * DEPTH)]
        sh_done, silu3_ready, hT3_ready = sem("sh_done"), sem("silu3_ready"), sem("hT3_ready")
        sh2_done, comb, ysel_free = sem("sh2_done"), sem("comb"), sem("ysel_free")
        stored = [sem(f"stored{b}") for b in range(2)]

        COMB_STEPS = 3 * DEPTH
        CREDIT = 1
        N_POOL_SETUP, N_DVE_SETUP, N_WEIGHTS, N_ZERO = 15, 17, 5, SLOTS * D // (P * 1024)

        def place(i, u, k):
            s = DEPTH * HEAD_ROUNDS + u - k
            return DEPTH * i + s, i + s // DEPTH, s % DEPTH

        def live(t):
            return not isinstance(t, int) or 0 <= t < TILES

        def past(t, lag):
            return not isinstance(t, int) or t >= lag

        def rounds(eng, step):
            for i in range(-HEAD_ROUNDS, 0):
                for u in range(DEPTH):
                    step(i, u)
            with eng.Fori(0, LOOPS) as i:
                for u in range(DEPTH):
                    step(i, u)
            for i in range(LOOPS, LOOPS + TAIL_ROUNDS):
                for u in range(DEPTH):
                    step(i, u)

        def tile_cols(t, n=P):
            return bass.ds(t * n, n)

        def pair_rounds(eng, step, depth):
            for u in range(DEPTH):
                step(0, u)
            with eng.Fori(1, EPAIRS // DEPTH) as i:
                for u in range(DEPTH):
                    step(i, u)
            for u in range(depth - 1):
                step(EPAIRS // DEPTH, u)

        def pair_place(i, u, k):
            return DEPTH * i + (u - k), i + (u - k) // DEPTH, (u - k) % DEPTH

        def pair_live(j):
            return not isinstance(j, int) or 0 <= j < EPAIRS

        block = ctx.enter_context(nc.Block())

        @block.sync
        def _(sp):
            for n, w in enumerate((Wq, Wk, Wv, Wo)):
                sp.dma_start(raw[:, n, :], w).then_inc(weights_in, 16)
            sp.dma_start(raw_gate[:, :], gate_w).then_inc(weights_in, 16)
            sp.dma_start(ids_i[:, :], x.rearrange("b (n p) -> (b n) p", p=P)).then_inc(ids_in, 16)
            sp.wait_ge(consts_ready, 1)
            rows = P * 1024 // D
            for n in range(N_ZERO):
                sp.dma_start(xslots[n * rows:(n + 1) * rows, :].rearrange("(p a) d -> p (a d)", p=P),
                             zeros[:, :]).then_inc(zeroed, 16)
            sp.dma_start(yslots[SLOTS:SLOTS + 1, :], zeros[0:1, 0:D]).then_inc(zeroed, 16)
            sp.dma_start(shared13[:, 0, :], sw1).then_inc(shared_in, 16)
            sp.dma_start(shared13[:, 1, :], sw3).then_inc(shared_in, 16)
            sp.dma_start(shared2[:, :], sw2).then_inc(shared_in, 16)

            def load_weights(j, r):
                sp.dma_start(w13[:, r, :, 0, :], w1[bass.ds(j * 2, 2)].rearrange("e d h -> d e h")).then_inc(w_in[r], 16)
                sp.dma_start(w13[:, r, :, 1, :], w3[bass.ds(j * 2, 2)].rearrange("e d h -> d e h")).then_inc(w_in[r], 16)
                sp.dma_start(w2s[:, r, :], w2[bass.ds(j * 2, 2)].rearrange("e h d -> (e h) d")).then_inc(w_in[r], 16)

            def load_slots(j, r):
                sp.dma_start(xs[:, r, :].rearrange("p (e f) -> p e f", e=2),
                             xslots[bass.ds(j * (2 * CAP), 2 * CAP), :].rearrange("(e p i) d -> p e (i d)", e=2, i=2)
                             ).then_inc(xs_in[r], 16)

            for r in range(DEPTH):
                load_weights(r, r)

            def step(i, u):
                t, q, r = place(i, u, NORM1)
                if live(t):
                    sp.wait_ge(gathered[r], 16 * (q + 1))
                    sp.dma_start(hres[:, tile_cols(t)], hg[:, r, :]).then_inc(res_saved[r], 16)
                t, q, r = place(i, u, GATE)
                if live(t):
                    sp.wait_ge(mix_ready, t + 3)
                    sp.dma_start(x2T_all[:, tile_cols(t)], mixT[:, r % 2, 1, :]).then_inc(x2T_saved[r % 2], 16)

            rounds(sp, step)
            for r in range(DEPTH):
                sp.wait_ge(scattered[r], 32 * (TILES // DEPTH))
            for r in range(DEPTH):
                load_slots(r, r)

            def store_y(j, r):
                sp.wait_ge(y_ready, 2 * (j + 1))
                sp.dma_start(yslots[bass.ds(j * (2 * CAP), 2 * CAP), :].rearrange("(e p i) d -> p e (i d)", e=2, i=2),
                             ys[:, r, :].rearrange("p (e f) -> p e f", e=2)).then_inc(y_out[r], 16)

            def refill(j, r):
                if not isinstance(j, int) or j + DEPTH < EPAIRS:
                    sp.wait_ge(xsT_done, j + 1)
                    load_slots(j + DEPTH, r)
                if not isinstance(j, int) or 2 <= j < EPAIRS - 2:
                    sp.wait_ge(y_done, j - 1)
                    load_weights(j + 2, (r + 2) % DEPTH)
                if not isinstance(j, int) or j >= 3:
                    store_y(j - 3, (r - 3) % DEPTH)

            for r in range(DEPTH):
                refill(r, r)
            with sp.Fori(1, EPAIRS // DEPTH - 1) as i:
                for r in range(DEPTH):
                    refill(DEPTH * i + r, r)
            for r in range(DEPTH):
                refill(EPAIRS - DEPTH + r, r)
            for j in range(EPAIRS - 3, EPAIRS):
                store_y(j, j % DEPTH)

            with sp.Fori(0, TILES // (2 * DEPTH)) as g:
                for b in range(2):
                    sp.wait_ge(comb, CREDIT + COMB_STEPS * (2 * g + b + 1))
                    sp.dma_start(out_rows[bass.ds((2 * g + b) * (DEPTH * P), DEPTH * P), :].rearrange("(n p) d -> p n d", p=P),
                                 acc[b].rearrange("p (n d) -> p n d", d=D)).then_inc(stored[b], 16)
            for b in range(2):
                sp.wait_ge(stored[b], CREDIT + 16 * (TILES // (2 * DEPTH)))
            sp.wait_ge(zeroed, 16 * (N_ZERO + 1))

        @block.gpsimd
        def _(pool):
            done = [0]

            def link(ins):
                done[0] += 1
                ins.then_inc(pool_setup, 1)
                pool.wait_ge(pool_setup, done[0])

            pool.memset(zeros[:, :], 0.0).then_inc(consts_ready, 1)
            link(pool.memset(ident[:, :], 0.0))
            link(pool.affine_select(out=ident[:, :], in_=ident[:, :], compare_op=ALU.not_equal, fill=1.0, base=0,
                                    pattern=[[-1, P]], channel_multiplier=1))
            link(pool.memset(onesb[:, :], 1.0))
            link(pool.affine_select(out=before[:, :], in_=onesb[:, :], compare_op=ALU.is_ge, fill=0.0, base=-1,
                                    pattern=[[1, P]], channel_multiplier=-1))
            link(pool.memset(masks[:, :], 0.0))
            for half in range(2):
                rows = slice(half * W, half * W + W)
                for c in (P, 2 * P):
                    pool.affine_select(out=masks[rows, c:c + W], in_=masks[rows, c:c + W], compare_op=ALU.is_ge,
                                       fill=MASKED, base=-1, pattern=[[1, W]], channel_multiplier=-1)
                for c in (W, P + W, 2 * P + W):
                    mask_ins = pool.affine_select(out=masks[rows, c:c + W], in_=masks[rows, c:c + W], compare_op=ALU.is_ge,
                                                  fill=MASKED, base=0, pattern=[[-1, W]], channel_multiplier=1)
                link(mask_ins)
            link(pool.memset(masks[:, 0:W], MASKED))
            link(pool.iota(expert_noi[:, :], pattern=[[1, E]], base=0, channel_multiplier=0))
            link(pool.memset(neghalf[:, :], -0.5))
            link(pool.memset(epscol[:, :], EPS))
            link(pool.memset(zero_i[:, :], 0))
            link(pool.memset(count[:, :], 0.0))
            link(pool.memset(base[:, :], 0.0))
            link(pool.memset(xnT[:, :], 0.0))
            assert done[0] == N_POOL_SETUP

            def step(i, u):
                t, q, r = place(i, u, GATHER)
                if live(t):
                    pool.wait_ge(id_picked, t + 1)
                    if past(t, DEPTH):
                        pool.wait_ge(xn_ready, t - DEPTH + 1)
                        pool.wait_ge(res_saved[r], 16 * q)
                t, q, r = place(i, u, SCATTER)
                if live(t):
                    pool.wait_ge(slot_ready, t + 1)
                    if isinstance(t, int) and t == 0:
                        pool.wait_ge(zeroed, 16 * (N_ZERO + 1))
                a, _, ar = place(i, u, NORM1)
                b, _, _ = place(i, u, NORM2)
                if live(a) or live(b):
                    lo, hi = (0 if live(a) else 1), (2 if live(b) else 1)
                    if live(a):
                        pool.wait_ge(aggr1, a + 1)
                    if live(b):
                        pool.wait_ge(aggr2, b + 1)
                    pool.tensor_tensor(rs[:, ar % 2, 0, lo:hi], mv[:, ar % 2, lo:hi, 1], epscol[:, lo:hi],
                                       ALU.add).then_inc(var_ready, 1)
                    pool.wait_ge(var_ready, a + 1)
                    pool.tensor_tensor(rs[:, ar % 2, 1, lo:hi], rs[:, ar % 2, 0, lo:hi], neghalf[:, lo:hi],
                                       ALU.pow).then_inc(rstd, 1)
                t, q, r = place(i, u, SCATTER)
                if live(t):
                    pool.wait_ge(rank_done, t + 1)
                    pool.tensor_tensor(count[:, :], count[:, :], pick[:, r % 2, 0, :], ALU.add).then_inc(counted_first, 1)
                    pool.wait_ge(counted_first, t + 1)
                    pool.tensor_tensor(count[:, :], count[:, :], pick[:, r % 2, 1, :], ALU.add).then_inc(counted, 1)
                t, q, r = place(i, u, GATHER)
                if live(t):
                    pool.indirect_dma_start(out=hg[:, r, :], out_offset=None, in_=tok_w[:, :],
                                            in_offset=bass.IndirectOffsetOnAxis(ap=row_id[:, r:r + 1], axis=0)
                                            ).then_inc(gathered[r], 16)
                t, q, r = place(i, u, SCATTER)
                if live(t):
                    for k in range(2):
                        pool.indirect_dma_start(out=xslots[:, :],
                                                out_offset=bass.IndirectOffsetOnAxis(ap=slot[:, r, k:k + 1], axis=0),
                                                in_=x2[:, r, :], in_offset=None, bounds_check=SLOTS - 1,
                                                oob_is_err=False).then_inc(scattered[r], 16)

            rounds(pool, step)

            for r in range(DEPTH):
                pool.wait_ge(y_out[r], CREDIT + 16 * (EPAIRS // DEPTH))
            with pool.Fori(0, TILES // (2 * DEPTH)) as g:
                for b in range(2):
                    pool.wait_ge(slots_now, 2 * g + b + 1)
                    pool.wait_ge(ysel_free, CREDIT + 2 * g + b)
                    pool.tensor_tensor(slot_now[:, b, :], slot_next[:, b, :], zero_i[:, :], ALU.add).then_inc(slots_taken, 1)
                    pool.wait_ge(slots_taken, 2 * g + b + 1)
                    pool.tensor_tensor(gate_scratch[:, :], neghalf[:, 0:1], epscol[:, 0:1], ALU.add)
                    for n in range(DEPTH):
                        m = b * DEPTH + n
                        for k in range(2):
                            pool.indirect_dma_start(
                                out=ysel[:, m, k, :], out_offset=None, in_=yslots[:, :],
                                in_offset=bass.IndirectOffsetOnAxis(ap=slot_now[:, b, 2 * n + k:2 * n + k + 1], axis=0)
                            ).then_inc(y_got[m], 16)

        @block.tensor
        def _(pe):
            pe.wait_ge(pool_setup, N_POOL_SETUP)
            pe.wait_ge(weights_in, 16 * N_WEIGHTS)
            for n in range(3):
                pe.transpose(ps[:, 0, n * P:(n + 1) * P], raw[:, n, :], ident[:, :])
            pe.transpose(ps[:, 2, 0:E], raw_gate[:, :], ident[0:E, 0:E]).then_inc(setup_T, 1)
            pe.wait_ge(dve_setup, 2)
            pe.transpose(ps[:, 1, 0:P], wo_perm[:, :], ident[:, :])
            pe.transpose(ps[:, 3, 0:TILES], ids_f[:, :], ident[0:TILES, 0:TILES]).then_inc(setup_T, 1)
            pe.wait_ge(dve_setup, N_DVE_SETUP)

            def score(i, u, half):
                t, q, r = place(i, u, SCORE)
                if not live(t):
                    return
                pe.wait_ge(qk_ready, t + 1)
                c = P
                if r == 0:
                    start = (t % SEQ_TILES == 0) if isinstance(t, int) else (i & 1)
                    c = P - start * P
                pairs = (2 * half, 2 * half + 1)
                for pair in pairs:
                    pe.matmul(S(pair), identb[:, :], masks[:, bass.ds(c, 2 * P)], start=True, stop=False)
                for blk in range(2):
                    for pair in pairs:
                        rows = slice(32 * pair, 32 * pair + 32)
                        c0 = r * P + blk * W
                        mm = pe.matmul(S(pair)[:, blk * P:(blk + 1) * P],
                                       QT[rows, r % 2, blk, :, :].rearrange("p a q -> p (a q)"), KT[rows, c0:c0 + P],
                                       start=False, stop=(blk == 1))
                mm.then_inc(s_done[half], 1)

            def turn_probs(t, r, half):
                pe.wait_ge(p_ready[half], t + 1)
                if past(t, 1):
                    pe.wait_ge(pT_ready[half], t)
                for n in range(4):
                    mm = pe.transpose(PT(half)[:, n * P:(n + 1) * P], prob[:, r % 2, half, n * P:(n + 1) * P], ident[:, :])
                mm.then_inc(pT_done[half], 1)

            def step(i, u):
                c, _, cr = place(i, u, PROJ)
                e, _, er = place(i, u, VALUE)
                f, _, fr = place(i, u, OUTP)
                g, _, gr = place(i, u, GATE)
                h, _, hr = place(i, u, ROUTE)

                if live(c - 1):
                    pe.wait_ge(qk_ready, c)
                if live(g - 1):
                    pe.wait_ge(elog_ready, g)
                if live(f):
                    pe.wait_ge(attn_ready, f + 1)
                    for blk in range(2):
                        mm = pe.matmul(p_fold[:, blk * W:(blk + 1) * W], attn[:, fr % 2, blk, :], fold2[:, :],
                                       start=True, stop=True)
                    mm.then_inc(fold_done, 1)
                if live(c):
                    pe.wait_ge(xn_ready, c + 1)
                    pe.transpose(p_xT, xn[:, cr % 2, :], ident[:, :]).then_inc(xT_done, 1)
                if live(g):
                    pe.wait_ge(x2_ready, g + 1)
                    pe.transpose(p_x2T, x2[:, gr, :], ident[:, :]).then_inc(x2T_done, 1)

                if live(e):
                    if live(c - 1):
                        pe.wait_ge(v_ready, c)
                    turn_probs(e, er, 0)
                score(i, u, 0)

                if live(c):
                    pe.wait_ge(xT_ready, c + 1)
                if live(f) or live(g):
                    pe.wait_ge(mix_ready, f + 1)
                if live(c):
                    cur = xnT[:, W + (cr % 2) * P:W + (cr % 2) * P + P]
                    pe.matmul(p_q, WqT[:, :], cur, start=True, stop=True)
                    pe.matmul(p_k, WkT[:, :], cur, start=True, stop=True).then_inc(qk_done, 1)
                if live(g):
                    pe.matmul(p_log, mixT[:, gr % 2, 1, :], gateT[:, :], start=True, stop=True).then_inc(log_done, 1)

                if live(e - 1):
                    pe.wait_ge(attn_ready, e)
                else:
                    if live(f - 1):
                        pe.wait_ge(res_ready, f)
                    if live(h - 1):
                        pe.wait_ge(rank_read, h)
                if live(f):
                    pe.matmul(p_wo, mixT[:, fr % 2, 0, :], WoT[:, :], start=True, stop=True).then_inc(wo_done, 1)
                if live(h):
                    pe.wait_ge(pick_ready, h + 1)
                    if past(h, 1):
                        pe.wait_ge(counted, h)
                    pe.matmul(p_rank, onesb[:, :], base[:, :], start=True, stop=False)
                    pe.matmul(p_rank, onesb[:, :], count[:, :], start=False, stop=False)
                    pe.matmul(p_rank, before[:, :], pick[:, hr % 2, 0, :], start=False, stop=False)
                    pe.matmul(p_rank, before[:, :], pick[:, hr % 2, 1, :], start=False, stop=True).then_inc(rank_done, 1)

                if live(e):
                    turn_probs(e, er, 1)

                if live(c):
                    if live(e):
                        pe.wait_ge(pT_ready[0], e + 1)
                    for blk in range(2):
                        c0 = (cr % 2) * P + blk * W
                        mm = pe.matmul(p_v[:, blk * P:(blk + 1) * P], xnT[:, c0:c0 + P], WvT[:, :], start=True, stop=True)
                    mm.then_inc(v_done, 1)

                if live(e):
                    if live(f):
                        pe.wait_ge(res_ready, f + 1)
                    if live(h):
                        pe.wait_ge(rank_read, h + 1)
                    pe.wait_ge(v_ready, e + 1)
                    for half in range(2):
                        pe.wait_ge(pT_ready[half], e + 1)
                        for n in range(2):
                            for blk in range(2):
                                pair = 2 * half + n
                                o0 = (blk * PAIRS + pair) * VW
                                k0 = (2 * n + blk) * P
                                mm = pe.matmul(p_o[:, o0:o0 + VW], probT[:, half, k0:k0 + P],
                                               V[:, er, blk, pair * VW:(pair + 1) * VW], start=True, stop=True)
                    mm.then_inc(o_done, 1)

                score(i, u, 1)

            rounds(pe, step)

            pe.wait_ge(attn_ready, TILES)

            def pair_step(i, u):
                j, q, r = pair_place(i, u, 0)
                if pair_live(j):
                    pe.wait_ge(xs_in[r], 16 * (q + 1))
                    if past(j, 2):
                        pe.wait_ge(xsT_ready, j - 1)
                    for s in range(4):
                        mm = pe.transpose(ps[:, r % 2, s * P:(s + 1) * P], xs[:, r, s * P:(s + 1) * P], ident[:, :])
                    mm.then_inc(xsT_done, 1)
                j, q, r = pair_place(i, u, 1)
                if pair_live(j):
                    pe.wait_ge(w_in[r], 48 * (q + 1))
                    pe.wait_ge(xsT_ready, j + 1)
                    if past(j, 2):
                        pe.wait_ge(hid_ready, j - 1)
                    for s in range(4):
                        mm = pe.matmul(ps[:, 2 + r % 2, s * P:(s + 1) * P], xsT[:, r % 2, s * P:(s + 1) * P],
                                       w13[:, r, s // 2, :, :], start=True, stop=True)
                    mm.then_inc(up_done, 1)
                j, q, r = pair_place(i, u, 2)
                if pair_live(j):
                    pe.wait_ge(hid_ready, j + 1)
                    if past(j, 1):
                        pe.wait_ge(hidT_ready, j)
                    for n in range(2):
                        mm = pe.transpose(ps[:, 4, n * P:(n + 1) * P],
                                          hid[:, r % 2, n, :, :].rearrange("p e h -> p (e h)"), ident[:, :])
                    mm.then_inc(hidT_done, 1)
                j, q, r = pair_place(i, u, 3)
                if pair_live(j):
                    pe.wait_ge(hidT_ready, j + 1)
                    if past(j, 1):
                        pe.wait_ge(y_ready, 2 * j)
                    for n in range(2):
                        for e in range(2):
                            rows = slice(e * H, (e + 1) * H)
                            c = (r % 2) * 2 * P + n * P
                            mm = pe.matmul(ps[:, 5 + e, c:c + P], hidT[rows, r % 2, n * P:(n + 1) * P],
                                           w2s[rows, r, :], start=True, stop=True)
                    mm.then_inc(y_done, 1)

            pair_rounds(pe, pair_step, 4)

            pe.wait_ge(shared_in, 48)
            for b in range(2):
                pe.wait_ge(x2T_saved[b], 16 * (TILES // 2))
            pe.wait_ge(y_ready, 2 * EPAIRS)
            with pe.Fori(0, TILES // (2 * DEPTH)) as g:
                for b in range(2):
                    pe.wait_ge(hT3_ready, CREDIT + 2 * g + b)
                    cols = bass.ds((2 * g + b) * (DEPTH * P), DEPTH * P)
                    for n in range(2):
                        mm = pe.matmul(ps[:, n, :], shared13[:, n, :], x2T_all[:, cols], start=True, stop=True)
                    mm.then_inc(sh_done, 1)
                    pe.wait_ge(hT3_ready, CREDIT + 2 * g + b + 1)
                    pe.wait_ge(comb, CREDIT + COMB_STEPS * (2 * g + b))
                    for n in range(DEPTH):
                        mm = pe.matmul(ps[:, 2, n * P:(n + 1) * P], hT3[b][:, n * P:(n + 1) * P], shared2[:, :],
                                       start=True, stop=True)
                    mm.then_inc(sh2_done, 1)

        @block.vector
        def _(dve):
            done = [0]

            def link(ins):
                done[0] += 1
                ins.then_inc(dve_setup, 1)
                dve.wait_ge(dve_setup, done[0])

            dve.wait_ge(weights_in, 16 * N_WEIGHTS)
            dve.wait_ge(ids_in, 16)
            link(dve.tensor_copy(wo_perm[:, :].rearrange("o (a b d) -> o a b d", a=2, b=PAIRS),
                                 raw[:, 3, :].rearrange("o (b a d) -> o a b d", a=2, b=PAIRS)))
            link(dve.tensor_copy(ids_f[:, :], ids_i[:, :]))
            dve.wait_ge(setup_T, 1)
            for n, wT in enumerate((WqT, WkT, WvT)):
                link(dve.tensor_copy(wT[:, :], ps[:, 0, n * P:(n + 1) * P]))
            link(dve.tensor_copy(gateT[:, :], ps[:, 2, 0:E]))
            dve.wait_ge(setup_T, 2)
            dve.tensor_copy(idsT[:, :], ps[:, 3, 0:TILES])
            link(dve.tensor_copy(WoT[:, :], ps[:, 1, 0:P]))
            dve.wait_ge(pool_setup, N_POOL_SETUP)
            link(dve.tensor_scalar(limit_of[:, :], expert_noi[:, :], float(CAP), float(CAP), ALU.mult, ALU.add))
            link(dve.tensor_scalar(base[0:1, :], limit_of[0:1, :], float(CAP), None, ALU.subtract))
            link(dve.tensor_copy(identb[:, :], ident[:, :]))
            link(dve.tensor_tensor(fold2[:, :], ident[:, 0:W], ident[:, W:2 * W], ALU.add))
            view = ident[:, :].rearrange("p (g c) -> p g c", c=2 * HD)
            for a in range(2):
                link(dve.tensor_reduce(qscale[:, a:a + 1], view[:, :, a * HD:(a + 1) * HD], AX.XY, ALU.add))
            link(dve.tensor_scalar(qscale[:, :], qscale[:, :], -SCALE, None, ALU.mult))
            link(dve.memset(attn[:, :, :, :], 0.0))
            link(dve.memset(V[:, :, :, :], 1.0))
            link(dve.memset(KT[:, :], 0.0))
            assert done[0] == N_DVE_SETUP

            def row_low(t, r, half):
                if live(t):
                    dve.wait_ge(s_done[half], t + 1)
                    scores = ps[:, 2 * half:2 * half + 2, 0:2 * P].rearrange("p n (b k) -> p n b k", b=2)
                    dve.tensor_reduce(low[:, r % 2, 2 * half:2 * half + 2, :], scores, AX.X, ALU.min
                                      ).then_inc(low_ready[half], 1)

            def step(i, u):
                gt, gq, gr = place(i, u, GATHER)
                at, aq, ar = place(i, u, NORM1)
                bt, bq, br = place(i, u, NORM2)
                et, _, er = place(i, u, VALUE)
                t, q, r = place(i, u, ROUTE)
                b = r % 2
                ab = ar % 2
                if live(gt):
                    if past(gt, DEPTH):
                        dve.wait_ge(gathered[gr], 16 * gq)
                    dve.tensor_copy(row_id[:, gr:gr + 1], idsT[:, bass.ds(gt, 1)]).then_inc(id_picked, 1)
                if live(at):
                    dve.wait_ge(gathered[ar], 16 * (aq + 1))
                if live(bt):
                    dve.wait_ge(res_ready, bt + 1)
                if live(t):
                    dve.wait_ge(elog_ready, t + 1)
                    dve.tensor_scalar(negd[:, :], elog[:, b, :], -1.0, -1.0, ALU.mult, ALU.add).then_inc(negd_ready, 1)
                if live(at):
                    dve.bn_stats(st1[:, :], hg[:, ar, :]).then_inc(stats1, 1)
                if live(bt):
                    dve.bn_stats(st2[:, :], hres[:, tile_cols(bt)]).then_inc(stats2, 1)
                    dve.wait_ge(stats2, bt + 1)
                if live(at):
                    dve.wait_ge(stats1, at + 1)
                if live(t):
                    dve.wait_ge(negd_ready, t + 1)
                row_low(et, er, 1)
                if live(at):
                    dve.bn_aggr(mv[:, ab, 0, :], st1[:, :]).then_inc(aggr1, 1)
                if live(bt):
                    dve.bn_aggr(mv[:, ab, 1, :], st2[:, :]).then_inc(aggr2, 1)
                if live(t):
                    dve.max(top[:, :], negd[:, :]).then_inc(top_ready, 1)
                    dve.wait_ge(top_ready, t + 1)
                    dve.tensor_copy(top_all[:, tile_cols(t, 2)], top[:, 0:2]).then_inc(top_saved, 1)
                    dve.max_index(topi[:, :], top[:, :], negd[:, :]).then_inc(topi_ready, 1)
                    dve.wait_ge(topi_ready, t + 1)
                    dve.tensor_scalar(limit[:, :], topi[:, 0:2], float(CAP), float(CAP), ALU.mult, ALU.add).then_inc(limit_ready, 1)
                    dve.wait_ge(limit_ready, t + 1)
                    if past(t, 2):
                        dve.wait_ge(counted, t - 1)
                    dve.tensor_tensor(pick[:, b, :, :], limit_of[:, :].unsqueeze(1).to_broadcast([P, 2, E]),
                                      limit[:, :].unsqueeze(2).to_broadcast([P, 2, E]), ALU.is_equal).then_inc(pick_ready, 1)
                st, _, sr = place(i, u, SCORE)
                row_low(st, sr, 0)
                t, q, r = place(i, u, NORM1)
                if live(t):
                    dve.wait_ge(rstd, t + 1)
                    if past(t, 2):
                        dve.wait_ge(xT_done, t - 1)
                    dve.tensor_scalar(xn[:, r % 2, :], hg[:, r, :], mv[:, r % 2, 0, 0:1], rs[:, r % 2, 1, 0:1], ALU.subtract,
                                      ALU.mult).then_inc(xn_ready, 1)
                t, q, r = place(i, u, NORM2)
                if live(t):
                    dve.wait_ge(rstd, t + NORM2 - NORM1 + 1)
                    if past(t, DEPTH):
                        dve.wait_ge(x2T_done, t - DEPTH + 1)
                        dve.wait_ge(scattered[r], 32 * q)
                    dve.tensor_scalar(x2[:, r, :], hres[:, tile_cols(t)], mv[:, r % 2, 1, 0:1], rs[:, r % 2, 1, 1:2], ALU.subtract,
                                      ALU.mult).then_inc(x2_ready, 1)
                h, _, hr = place(i, u, ROUTE)
                t, q, r = place(i, u, OUTP)
                if live(h):
                    dve.wait_ge(rank_done, h + 1)
                if live(t):
                    dve.wait_ge(wo_done, t + 1)
                    dve.wait_ge(res_saved[r], 16 * (q + 1))
                    dve.tensor_tensor(hres[:, tile_cols(t)], p_wo, hres[:, tile_cols(t)], ALU.add).then_inc(res_ready, 1)
                if live(h):
                    dve.tensor_tensor(rank[:, :, :], p_rank.unsqueeze(1).to_broadcast([P, 2, E]), pick[:, hr % 2, :, :],
                                      ALU.mult).then_inc(rank_read, 1)
                    dve.wait_ge(rank_read, h + 1)
                    dve.tensor_reduce(seat[:, :], rank[:, :, :], AX.X, ALU.add).then_inc(seat_ready, 1)
                    dve.wait_ge(seat_ready, h + 1)
                    dve.tensor_tensor(over[:, :], seat[:, :], limit[:, :], ALU.is_ge).then_inc(over_ready, 1)
                    dve.wait_ge(over_ready, h + 1)
                    dve.scalar_tensor_tensor(slot[:, hr, :], over[:, :], float(2 * SLOTS), seat[:, :], ALU.mult,
                                             ALU.add).then_inc(slot_ready, 1)
                t, q, r = place(i, u, VALUE)
                if live(t):
                    dve.wait_ge(o_done, t + 1)
                    o = p_o.rearrange("p (b g c) -> p b g c", b=2, c=VW)
                    rr = rsum[:, r % 2, :].rearrange("p (b g) -> p b g", b=2)
                    dve.reciprocal(rr, o[:, :, :, 2 * HD]).then_inc(rsum_ready, 1)
                    if live(h) and hr == DEPTH - 1:
                        dve.wait_ge(slot_ready, h + 1)
                        dve.tensor_scalar(slot_all[:, bass.ds((h - hr) * 2, 2 * DEPTH)],
                                          slot[:, :, :].rearrange("p t k -> p (t k)"), float(SLOTS), None, ALU.min
                                          ).then_inc(slots_saved, 1)
                    dve.wait_ge(rsum_ready, t + 1)
                    if past(t, 2):
                        dve.wait_ge(fold_done, t - 1)
                    for a in range(2):
                        rows = slice(a * W, (a + 1) * W)
                        ins = dve.tensor_tensor(
                            attn[rows, r % 2, :, a * W:(a + 1) * W].rearrange("p b (g d) -> p b g d", d=HD),
                            o[rows, :, :, a * HD:(a + 1) * HD],
                            rr[rows].unsqueeze(3).to_broadcast([W, 2, PAIRS, HD]), ALU.mult)
                    ins.then_inc(attn_ready, 1)
                elif live(h) and hr == DEPTH - 1:
                    dve.wait_ge(slot_ready, h + 1)
                    dve.tensor_scalar(slot_all[:, bass.ds((h - hr) * 2, 2 * DEPTH)],
                                      slot[:, :, :].rearrange("p t k -> p (t k)"), float(SLOTS), None, ALU.min
                                      ).then_inc(slots_saved, 1)

            rounds(dve, step)

            dve.wait_ge(top_saved, TILES)
            dve.reciprocal(best_all[:, :], top_all[:, :]).then_inc(gains, 1)
            dve.wait_ge(gains, 1)
            best = best_all[:, :].rearrange("p (t k) -> p t k", k=2)
            dve.scalar_tensor_tensor(sum_all[:, :], best[:, :, 0], -1e-20, best[:, :, 1], ALU.add, ALU.add).then_inc(gains, 1)
            dve.wait_ge(gains, 2)
            dve.reciprocal(inv_all[:, :], sum_all[:, :]).then_inc(gains, 1)
            dve.wait_ge(gains, 3)
            dve.scalar_tensor_tensor(gain_all[:, :].rearrange("p (t k) -> p t k", k=2), best, ROUTE_SCALE,
                                     inv_all[:, :].unsqueeze(2).to_broadcast([P, TILES, 2]), ALU.mult, ALU.mult
                                     ).then_inc(gains, 1)
            dve.wait_ge(gains, 4)
            dve.wait_ge(slots_saved, TILES // DEPTH)

            for s in y_out:
                dve.engine_nop().then_inc(s, CREDIT)

            def pair_step(i, u):
                j, q, r = pair_place(i, u, 1)
                if pair_live(j):
                    b = r % 2
                    up = ps[:, 2 + b, :].rearrange("p (s a h) -> p s a h", s=4, a=2)
                    dve.wait_ge(silu_ready, j + 1)
                    if past(j, 2):
                        dve.wait_ge(hidT_done, j - 1)
                    dve.tensor_tensor(hid[:, b, :, :, :].rearrange("p n e h -> p e n h"),
                                      up[:, :, 1, :].rearrange("p (e n) h -> p e n h", e=2),
                                      silu[:, b, :, :].rearrange("p (e n) h -> p e n h", e=2),
                                      ALU.mult).then_inc(hid_ready, 1)
                j, q, r = pair_place(i, u, 3)
                if pair_live(j):
                    dve.wait_ge(y_done, j + 1)
                    if past(j, DEPTH):
                        dve.wait_ge(y_out[r], CREDIT + 16 * q)
                    dve.tensor_copy(ys[:, r, 0:2 * P], ps[:, 5, (r % 2) * 2 * P:(r % 2 + 1) * 2 * P]).then_inc(y_ready, 1)

            pair_rounds(dve, pair_step, 4)

            for b in range(2):
                dve.tensor_copy(slot_next[:, b, :], slot_all[:, b * 2 * DEPTH:(b + 1) * 2 * DEPTH]).then_inc(slots_now, 1)
            for s in (hT3_ready, comb, *stored):
                dve.engine_nop().then_inc(s, CREDIT)
            for b in range(2):
                dve.engine_nop().then_inc(ysel_free, 1)
            with dve.Fori(0, TILES // (2 * DEPTH)) as g:
                for b in range(2):
                    gg = 2 * g + b
                    dve.wait_ge(silu3_ready, gg + 1)
                    dve.tensor_tensor(hT3[b], ps[:, 1, :], silu3[b], ALU.mult).then_inc(hT3_ready, 1)
                    dve.wait_ge(sh2_done, gg + 1)
                    dve.wait_ge(stored[b], CREDIT + 16 * g)
                    for n in range(DEPTH):
                        m = b * DEPTH + n
                        a = acc[b][:, n * P:(n + 1) * P]
                        t = gg * DEPTH + n
                        c = COMB_STEPS * gg + 3 * n
                        dve.tensor_tensor(a, ps[:, 2, n * P:(n + 1) * P], hres[:, tile_cols(t)], ALU.add).then_inc(comb, 1)
                        dve.wait_ge(y_got[m], 32 * (g + 1))
                        for k in range(2):
                            dve.wait_ge(comb, CREDIT + c + k + 1)
                            ins = dve.scalar_tensor_tensor(a, ysel[:, m, k, :], gain_all[:, bass.ds(2 * t + k, 1)], a,
                                                           ALU.mult, ALU.add).then_inc(comb, 1)
                    dve.wait_ge(comb, CREDIT + COMB_STEPS * (gg + 1))
                    dve.wait_ge(slots_taken, gg + 1)
                    nxt = (gg + 2) & (TILES // DEPTH - 1)
                    dve.tensor_copy(slot_next[:, b, :], slot_all[:, bass.ds(nxt * (2 * DEPTH), 2 * DEPTH)]).then_inc(slots_now, 1)
                    dve.engine_nop().then_inc(ysel_free, 1)

        @block.scalar
        def _(act):
            act.wait_ge(dve_setup, N_DVE_SETUP)

            def exps(t, r, half):
                if live(t):
                    act.wait_ge(low_ready[half], t + 1)
                    for n in range(2):
                        pair = 2 * half + n
                        for blk in range(2):
                            k0 = (2 * n + blk) * P
                            ins = act.activation(prob[:, r % 2, half, k0:k0 + P], S(pair)[:, blk * P:(blk + 1) * P], ACT.Exp,
                                                 bias=low[:, r % 2, pair, blk:blk + 1], scale=-1.0)
                    ins.then_inc(p_ready[half], 1)

            def copy_pT(i, u, half):
                t, q, r = place(i, u, VALUE)
                if live(t):
                    act.wait_ge(pT_done[half], t + 1)
                    if past(t, 1):
                        act.wait_ge(o_done, t)
                    act.copy(probT[:, half, :], PT(half)).then_inc(pT_ready[half], 1)

            def step(i, u):
                c, _, cr = place(i, u, PROJ)
                d, _, dr = place(i, u, SCORE)
                e, _, er = place(i, u, VALUE)
                f, _, fr = place(i, u, OUTP)
                g, gq, gr = place(i, u, GATE)
                if live(c):
                    act.wait_ge(xT_done, c + 1)
                    if past(c, 1):
                        act.wait_ge(v_done, c)
                        act.wait_ge(qk_done, c)
                if live(f):
                    act.wait_ge(fold_done, f + 1)
                    if past(f, 2):
                        act.wait_ge(wo_done, f - 1)
                if live(g):
                    act.wait_ge(x2T_done, g + 1)
                    if past(g, 2):
                        act.wait_ge(log_done, g - 1)
                        act.wait_ge(x2T_saved[gr % 2], 16 * (2 * gq + gr // 2))
                if live(c):
                    if cr % 2:
                        act.copy(xnT[:, 0:W], p_xT[:, W:P])
                    act.copy(xnT[:, W + (cr % 2) * P:W + (cr % 2 + 1) * P], p_xT).then_inc(xT_ready, 1)
                if live(f) or live(g):
                    lo, hi = (0 if live(f) else 1), (2 if live(g) else 1)
                    act.copy(mixT[:, fr % 2, lo:hi, :], p_mix.rearrange("p (n c) -> p n c", n=2)[:, lo:hi, :]
                             ).then_inc(mix_ready, 1)
                exps(e, er, 1)
                copy_pT(i, u, 0)
                exps(d, dr, 0)
                copy_pT(i, u, 1)
                if live(g):
                    act.wait_ge(log_done, g + 1)
                    if past(g, 2):
                        act.wait_ge(negd_ready, g - 1)
                if live(c):
                    act.wait_ge(qk_done, c + 1)
                    if past(c, 2):
                        act.wait_ge(s_done[1], c - 1)
                    for a in range(2):
                        act.activation(QT[:, cr % 2, :, a, :], p_q.rearrange("p (b q) -> p b q", b=2), ACT.Identity,
                                       scale=qscale[:, a:a + 1])
                    if cr == DEPTH - 1:
                        act.copy(KT[:, 0:W], p_k[:, W:P])
                    act.copy(KT[:, W + cr * P:W + (cr + 1) * P], p_k).then_inc(qk_ready, 1)
                if live(g):
                    act.activation(elog[:, gr % 2, :], p_log, ACT.Exp, scale=-1.0).then_inc(elog_ready, 1)
                if live(c):
                    act.wait_ge(v_done, c + 1)
                    if past(c, DEPTH):
                        act.wait_ge(o_done, c - DEPTH + 1)
                    act.copy(V[:, cr, :, :].rearrange("p b (g c) -> p b g c", c=VW)[:, :, :, 0:2 * HD],
                             p_v.rearrange("p (b g c) -> p b g c", b=2, c=2 * HD)).then_inc(v_ready, 1)

            rounds(act, step)

            def pair_step(i, u):
                j, q, r = pair_place(i, u, 0)
                if pair_live(j):
                    act.wait_ge(xsT_done, j + 1)
                    if past(j, 2):
                        act.wait_ge(up_done, j - 1)
                    act.copy(xsT[:, r % 2, :], ps[:, r % 2, :]).then_inc(xsT_ready, 1)
                j, q, r = pair_place(i, u, 1)
                if pair_live(j):
                    act.wait_ge(up_done, j + 1)
                    if past(j, 2):
                        act.wait_ge(hid_ready, j - 1)
                    act.activation(silu[:, r % 2, :, :],
                                   ps[:, 2 + r % 2, :].rearrange("p (s a h) -> p s a h", s=4, a=2)[:, :, 0, :],
                                   ACT.Silu).then_inc(silu_ready, 1)
                j, q, r = pair_place(i, u, 2)
                if pair_live(j):
                    act.wait_ge(hidT_done, j + 1)
                    if past(j, 2):
                        act.wait_ge(y_done, j - 1)
                    act.copy(hidT[:, r % 2, :], ps[:, 4, 0:2 * P]).then_inc(hidT_ready, 1)
                j, q, r = pair_place(i, u, 3)
                if pair_live(j):
                    act.wait_ge(y_done, j + 1)
                    if past(j, DEPTH):
                        act.wait_ge(y_out[r], CREDIT + 16 * q)
                    act.copy(ys[:, r, 2 * P:4 * P], ps[:, 6, (r % 2) * 2 * P:(r % 2 + 1) * 2 * P]).then_inc(y_ready, 1)

            pair_rounds(act, pair_step, 4)

            act.wait_ge(y_ready, 2 * EPAIRS)
            with act.Fori(0, TILES // (2 * DEPTH)) as g:
                for b in range(2):
                    act.wait_ge(sh_done, 2 * g + b + 1)
                    act.activation(silu3[b], ps[:, 0, :], ACT.Silu).then_inc(silu3_ready, 1)


_INS = ['x', 'L0_tok_w', 'L0_attn_Wq', 'L0_attn_Wk', 'L0_attn_Wv', 'L0_attn_Wo', 'L0_ffn_gate_w', 'L0_ffn_w1',
        'L0_ffn_w3', 'L0_ffn_w2', 'L0_ffn_sw1', 'L0_ffn_sw3', 'L0_ffn_sw2']
_OUTS = [((8, 1024, 128), 'float32')]


def kernel(**inputs):
    import numpy as _np
    import concourse.bacc as _bacc
    from concourse import mybir as _mybir
    from concourse.bass_utils import run_bass_kernel_spmd as _run

    nc = _bacc.Bacc("TRN2", target_bir_lowering=False, num_devices=1)
    arrays, args = {}, []
    for name in _INS:
        a = _np.ascontiguousarray(inputs[name])
        arrays[f"in_{name}_dram"] = a
        args.append(nc.dram_tensor(f"in_{name}_dram", a.shape, _mybir.dt.from_np(a.dtype), kind="ExternalInput").ap())
    for i, (shape, dtype) in enumerate(_OUTS):
        dt = _mybir.dt.from_np(_np.dtype(dtype))
        args.append(nc.dram_tensor(f"out_{i}_dram", shape, dt, kind="ExternalOutput").ap())
    lm_tower(nc, *args)
    r = _run(nc, [arrays], core_ids=[0])
    return r.results[0]["out_0_dram"]
```

```python
from contextlib import ExitStack

import concourse.bass as bass
from concourse import mybir

F32, BF16, I32, U32 = mybir.dt.float32, mybir.dt.bfloat16, mybir.dt.int32, mybir.dt.uint32
ALU = mybir.AluOpType
ACT = mybir.ActivationFunctionType
AX = mybir.AxisListType

P = 128
HEADS, HD = 8, 16
PAIRS = HEADS // 2
W = 64
EPS = 1e-5
SCALE = HD ** -0.5
MASKED = 1e30
CAP, ROUTE_SCALE = 256, 2.5
DEPTH = 4
HEAD_ROUNDS, TAIL_ROUNDS = 3, 3

GATHER, NORM1, PROJ, SCORE, VALUE, ATTN, OUTP, NORM2, GATE, ROUTE, SCATTER = range(11)

LOAD, UP, TURN, DOWN = range(4)
SHARED = 3


def lm_tower(nc, x, tok_w, Wq, Wk, Wv, Wo, gate_w, w1, w3, w2, sw1, sw3, sw2, out):
    BATCH, SEQ = x.shape
    E, D, H = w1.shape
    TILES = BATCH * SEQ // P
    SEQ_TILES = SEQ // P
    LOOPS = TILES // DEPTH - HEAD_ROUNDS
    EPAIRS = E // 2
    GROUPS = TILES // DEPTH
    SLOTS = E * CAP
    ROW = D + 4
    VW = 2 * HD + 1
    NO_ROW = 2 * BATCH * SEQ
    ZERO_ROUNDS = LOOPS + TAIL_ROUNDS
    YROWS = NO_ROW // ZERO_ROUNDS
    ZCOLS = 8 * ROW
    assert D == P and SEQ_TILES % 8 == 0 and 2 * H == P and E == W

    out_rows = out.rearrange("b s d -> (b s) d")
    xslots = nc.dram_tensor("xslots", [SLOTS, ROW], F32, kind="Internal").ap()
    ytok = nc.dram_tensor("ytok", [2 * BATCH * SEQ, D], F32, kind="Internal").ap()

    ctx = ExitStack()
    with ctx:
        def sb(name, shape, dt=F32):
            return ctx.enter_context(nc.sbuf_tensor(name, shape, dt))

        def sem(name):
            return ctx.enter_context(nc.semaphore(name))

        ident = sb("ident", [P, P])
        identb = sb("identb", [P, P], BF16)
        before = sb("before", [P, P], BF16)
        base = sb("base", [P, E], BF16)
        count = sb("count", [P, E], BF16)
        onesb = sb("onesb", [P, P], BF16)
        masks = sb("masks", [P, 2, 4, W], BF16)
        qscale = sb("qscale", [P, 2])
        tags = sb("tags", [P, 2 * TILES])
        tagsi = sb("tagsi", [P, TILES], I32)
        limit_of = sb("limit_of", [P, E])
        limit_at = sb("limit_at", [P, E, 2])
        row_noi = sb("row_noi", [P, 1], I32)
        row_no, query, key_no = sb("row_no", [P, 1]), sb("query", [P, 1]), sb("key_no", [P, W])
        expert_noi = sb("expert_noi", [P, E], I32)
        neghalf = sb("neghalf", [P, 2])
        epscol = sb("epscol", [P, 2])
        zeros = sb("zeros", [P, ZCOLS])
        raw = sb("raw", [P, 4, P])
        wo_perm = sb("wo_perm", [P, P])
        raw_gate = sb("raw_gate", [E, P])
        WqT, WkT, WvT, WoT = (sb(n, [P, P]) for n in ("WqT", "WkT", "WvT", "WoT"))
        gateT = sb("gateT", [P, E])
        shared13 = sb("shared13", [P, 2, P])
        shared2 = sb("shared2", [P, P])
        ids_i = sb("ids_i", [TILES, P], I32)
        ids_f = sb("ids_f", [TILES, P])
        idsT = sb("idsT", [P, TILES])

        hres = sb("hres", [P, TILES * P])
        x2T_all = sb("x2T_all", [P, TILES * P])
        top_all = sb("top_all", [P, 2 * TILES])
        best_all = sb("best_all", [P, 2 * TILES])
        sum_all, inv_all = sb("sum_all", [P, TILES]), sb("inv_all", [P, TILES])
        gain_all = sb("gain_all", [P, 2 * TILES])

        row_id = sb("row_id", [P, DEPTH], I32)
        hg = sb("hg", [P, DEPTH, P])
        st1, st2 = sb("st1", [P, 6]), sb("st2", [P, 6])
        mv = sb("mv", [P, 2, 2, 2])
        rs = sb("rs", [P, 2, 2, 2])
        xn = sb("xn", [P, 2, P])
        xnT = sb("xnT", [P, 2, P])
        KT = sb("KT", [P, 2, DEPTH, W])
        QT = sb("QT", [P, 2, 2, 2, W])
        V = sb("V", [P, DEPTH, 2, PAIRS * VW])
        low = sb("low", [P, 2, PAIRS, 2])
        prob = sb("prob", [P, 2, 2, 2 * 2 * P])
        probT = sb("probT", [P, 2, 2 * 2 * P])
        rsum = sb("rsum", [P, 2, 2 * PAIRS])
        attn = sb("attn", [P, 2, 2, P])
        mixT = sb("mixT", [P, 2, 2, P])
        x2 = sb("x2", [P, DEPTH, ROW])
        elog = sb("elog", [P, 2, E])
        negd = sb("negd", [P, E])
        top = sb("top", [P, 8])
        topi = sb("topi", [P, 8], U32)
        limit = sb("limit", [P, 3])
        pick = sb("pick", [P, 2, 2, E], BF16)
        rank = sb("rank", [P, 2, E])
        seat, over = sb("seat", [P, 2]), sb("over", [P, 2])
        slot = sb("slot", [P, DEPTH, 2], I32)

        xs = sb("xs", [P, DEPTH, 4, ROW])
        other = sb("other", [P, DEPTH, 4])
        row_f = sb("row_f", [P, DEPTH, 4])
        row_i = sb("row_i", [P, DEPTH, 4], I32)
        w13 = sb("w13", [P, DEPTH, 2, 2, H])
        w2s = sb("w2s", [P, DEPTH, P])
        xsT = sb("xsT", [P, 2, 4 * P])
        silu = sb("silu", [P, 2, 4, H])
        hid = sb("hid", [P, 2, 2, 2, H])
        hidT = sb("hidT", [P, 2, 2 * P])
        ys = sb("ys", [P, DEPTH, 4 * P])

        silu_sh, hid_sh = sb("silu_sh", [P, 2 * P]), sb("hid_sh", [P, 2 * P])
        wait_holder, warm = sb("wait_holder", [P, 1]), sb("warm", [P, 1])

        ysel = sb("ysel", [P, DEPTH, DEPTH, 2 * P])

        ps = ctx.enter_context(nc.psum_tensor("ps", [P, 8, 512], F32))

        def S(pair):
            return ps[:, pair, 0:2 * P]

        def PT(half):
            return ps[:, 4 + half, :]

        p_v = ps[:, 4, 0:P]
        p_xT, p_turn, p_x2T = ps[:, 6, 0:P], ps[:, 6, P:3 * P], ps[:, 6, 3 * P:4 * P]
        p_q, p_k, p_log = ps[:, 6, 0:P], ps[:, 6, P:2 * P], ps[:, 6, 2 * P:2 * P + E]
        p_wo, p_rank = ps[:, 7, 0:P], ps[:, 7, P:P + E]
        p_o = ps[:, 7, 0:2 * PAIRS * VW]

        consts_ready = sem("consts_ready")
        pool_setup = sem("pool_setup")
        dve_setup = sem("dve_setup")
        weights_in = sem("weights_in")
        ids_in = sem("ids_in")
        shared_in = sem("shared_in")
        setup_T, ids_ready, ids_T, wo_ready, act_setup = (
            sem("setup_T"), sem("ids_ready"), sem("ids_T"), sem("wo_ready"), sem("act_setup"))
        zeroed, ytok_zeroed = sem("zeroed"), sem("ytok_zeroed")
        id_picked = sem("id_picked")
        gathered = [sem(f"gathered{r}") for r in range(DEPTH)]
        res_saved = [sem(f"res_saved{r}") for r in range(DEPTH)]
        stats1, stats2, aggr1, aggr2 = sem("stats1"), sem("stats2"), sem("aggr1"), sem("aggr2")
        var_ready, rstd, xn_ready = sem("var_ready"), sem("rstd"), sem("xn_ready")
        xT_done, xT_ready = sem("xT_done"), sem("xT_ready")
        qk_done, qk_ready = sem("qk_done"), sem("qk_ready")
        v_done, v_ready = sem("v_done"), sem("v_ready")
        s_done, low_ready, p_ready, pT_done, pT_ready = (
            [sem(f"{name}{half}") for half in range(2)] for name in ("s_done", "low_ready", "p_ready", "pT_done", "pT_ready"))
        o_done, rsum_ready, attn_ready = sem("o_done"), sem("rsum_ready"), sem("attn_ready")
        turn_done, mix_ready = sem("turn_done"), sem("mix_ready")
        wo_done, res_ready = sem("wo_done"), sem("res_ready")
        x2_ready = sem("x2_ready")
        x2T_done, counted_first, counted = sem("x2T_done"), sem("counted_first"), sem("counted")
        x2T_saved = [sem(f"x2T_saved{b}") for b in range(2)]
        log_done, elog_ready = sem("log_done"), sem("elog_ready")
        negd_ready, top_ready, top_saved = sem("negd_ready"), sem("top_ready"), sem("top_saved")
        topi_ready, limit_ready, pick_ready = sem("topi_ready"), sem("limit_ready"), sem("pick_ready")
        rank_done, rank_read, seat_ready = sem("rank_done"), sem("rank_read"), sem("seat_ready")
        over_ready, slot_ready, gains = sem("over_ready"), sem("slot_ready"), sem("gains")
        scattered = [sem(f"scattered{r}") for r in range(DEPTH)]
        xs_in = [sem(f"xs_in{r}") for r in range(DEPTH)]
        w_in = [sem(f"w_in{r}") for r in range(DEPTH)]
        xsT_done, xsT_ready = sem("xsT_done"), sem("xsT_ready")
        up_done, silu_ready, hid_ready = sem("up_done"), sem("silu_ready"), sem("hid_ready")
        hidT_done, hidT_ready = sem("hidT_done"), sem("hidT_ready")
        y_done, y_ready = sem("y_done"), sem("y_ready")
        y_out = [sem(f"y_out{r}") for r in range(DEPTH)]
        other_ready, tags_read, row_ready = sem("other_ready"), sem("tags_read"), sem("row_ready")
        sh_up_done, sh_silu_ready, sh_hid_ready = sem("sh_up_done"), sem("sh_silu_ready"), sem("sh_hid_ready")
        sh_done, sh_added = sem("sh_done"), sem("sh_added")
        held = sem("held")
        y_in = [sem(f"y_in{r}") for r in range(DEPTH)]
        first_added, scaled, complete, stored = sem("first_added"), sem("scaled"), sem("complete"), sem("stored")

        N_IDENT, N_SMALL, N_POOL_SETUP, N_DVE_SETUP, N_WEIGHTS, N_ZERO = 2, 7, 9, 28, 5, SLOTS // (P * 8)

        def place(i, u, k):
            s = DEPTH * HEAD_ROUNDS + u - k
            return DEPTH * i + s, i + s // DEPTH, s % DEPTH

        def live(t):
            return not isinstance(t, int) or 0 <= t < TILES

        def past(t, lag):
            return not isinstance(t, int) or t >= lag

        def rounds(eng, step):
            for i in range(-HEAD_ROUNDS, 0):
                for u in range(DEPTH):
                    step(i, u)
            with eng.Fori(0, LOOPS) as i:
                for u in range(DEPTH):
                    step(i, u)
            for i in range(LOOPS, LOOPS + TAIL_ROUNDS):
                for u in range(DEPTH):
                    step(i, u)

        def tile_cols(t, n=P):
            return bass.ds(t * n, n)

        def pair_rounds(eng, step, depth):
            for u in range(DEPTH):
                step(0, u)
            with eng.Fori(1, EPAIRS // DEPTH) as i:
                for u in range(DEPTH):
                    step(i, u)
            for u in range(depth - 1):
                step(EPAIRS // DEPTH, u)

        def pair_place(i, u, k):
            return DEPTH * i + (u - k), i + (u - k) // DEPTH, (u - k) % DEPTH

        def pair_live(j):
            return not isinstance(j, int) or 0 <= j < EPAIRS

        block = ctx.enter_context(nc.Block())

        @block.sync
        def _(sp):
            sp.dma_start(ids_i[:, :], x.rearrange("b (n p) -> (b n) p", p=P)).then_inc(ids_in, 16)
            for n, w in enumerate((Wq, Wk, Wv, Wo)):
                sp.dma_start(raw[:, n, :], w).then_inc(weights_in, 16)
            sp.dma_start(raw_gate[:, :], gate_w).then_inc(weights_in, 16)
            sp.wait_ge(consts_ready, 1)

            def load_weights(j, r):
                sp.dma_start(w13[:, r, :, 0, :], w1[bass.ds(j * 2, 2)].rearrange("e d h -> d e h")).then_inc(w_in[r], 16)
                sp.dma_start(w13[:, r, :, 1, :], w3[bass.ds(j * 2, 2)].rearrange("e d h -> d e h")).then_inc(w_in[r], 16)
                sp.dma_start(w2s[:, r, :], w2[bass.ds(j * 2, 2)].rearrange("e h d -> (e h) d")).then_inc(w_in[r], 16)

            def load_slots(j, r):
                sp.dma_start(xs[:, r, :, :].rearrange("p (e i) f -> p e (i f)", e=2),
                             xslots[bass.ds(j * (2 * CAP), 2 * CAP), :].rearrange("(e p i) f -> p e (i f)", e=2, i=2)
                             ).then_inc(xs_in[r], 16)

            def step(i, u):
                t, q, r = place(i, u, NORM1)
                if live(t):
                    sp.wait_ge(gathered[r], 16 * (q + 1))
                    sp.dma_start(hres[:, tile_cols(t)], hg[:, r, :]).then_inc(res_saved[r], 16)
                t, q, r = place(i, u, GATE)
                if live(t):
                    sp.wait_ge(mix_ready, t + 3)
                    sp.dma_start(x2T_all[:, tile_cols(t)], mixT[:, r % 2, 1, :]).then_inc(x2T_saved[r % 2], 16)

                n = DEPTH * (i + HEAD_ROUNDS) + u - 1
                if isinstance(i, int) and 0 <= n < N_ZERO // 2:
                    for h in (2 * n, 2 * n + 1):
                        sp.dma_start(xslots[h * 8 * P:(h + 1) * 8 * P, :].rearrange("(p a) d -> p (a d)", p=P),
                                     zeros[:, :]).then_inc(zeroed, 16)
                if u == 0 and not (isinstance(i, int) and i < 0):
                    sp.dma_start(ytok[bass.ds(i * YROWS, YROWS), :].rearrange("(p a) d -> p (a d)", p=P),
                                 zeros[:, 0:YROWS * D // P]).then_inc(ytok_zeroed, 16)
                if isinstance(i, int) and i == -1 and u == DEPTH - 1:
                    sp.dma_start(shared13[:, 0, :], sw1).then_inc(shared_in, 16)
                    sp.dma_start(shared13[:, 1, :], sw3).then_inc(shared_in, 16)
                    sp.dma_start(shared2[:, :], sw2).then_inc(shared_in, 16)
                    for r in range(DEPTH):
                        load_weights(r, r)

            rounds(sp, step)
            for r in range(DEPTH):
                sp.wait_ge(scattered[r], 32 * (TILES // DEPTH))
            for r in range(DEPTH):
                load_slots(r, r)

            def refill(j, r):
                if not isinstance(j, int) or j + DEPTH < EPAIRS:
                    sp.wait_ge(xsT_done, j + 1)
                    sp.wait_ge(tags_read, j + 1)
                    load_slots(j + DEPTH, r)
                if not isinstance(j, int) or 2 <= j < EPAIRS - 2:
                    sp.wait_ge(y_done, j - 1)
                    load_weights(j + 2, (r + 2) % DEPTH)

            for r in range(DEPTH):
                refill(r, r)
            with sp.Fori(1, EPAIRS // DEPTH - 1) as i:
                for r in range(DEPTH):
                    refill(DEPTH * i + r, r)
            for r in range(DEPTH):
                refill(EPAIRS - DEPTH + r, r)

            def load_y(g, r):
                sp.dma_start(ysel[:, r, :, :],
                             ytok[bass.ds(g * (2 * DEPTH * P), 2 * DEPTH * P), :].rearrange("(n p k) d -> p n (k d)", p=P, k=2)
                             ).then_inc(y_in[r], 16)

            def store(g):
                sp.wait_ge(complete, g + 1)
                sp.dma_start(out_rows[bass.ds(g * (DEPTH * P), DEPTH * P), :].rearrange("(n p) d -> p n d", p=P),
                             hres[:, tile_cols(g, DEPTH * P)].rearrange("p (n d) -> p n d", d=D)).then_inc(stored, 16)

            for r in range(DEPTH):
                sp.wait_ge(y_out[r], 64 * (EPAIRS // DEPTH))
            for r in range(DEPTH):
                load_y(r, r)
            with sp.Fori(0, GROUPS // DEPTH - 1) as i:
                for r in range(DEPTH):
                    store(DEPTH * i + r)
                    load_y(DEPTH * (i + 1) + r, r)
            for r in range(DEPTH):
                store(GROUPS - DEPTH + r)
            sp.wait_ge(stored, 16 * GROUPS)
            sp.wait_ge(zeroed, 16 * N_ZERO)
            sp.wait_ge(ytok_zeroed, 16 * ZERO_ROUNDS)

        @block.gpsimd
        def _(pool):
            done = [0]

            def link(ins):
                done[0] += 1
                ins.then_inc(pool_setup, 1)
                pool.wait_ge(pool_setup, done[0])

            link(pool.memset(ident[:, :], 0.0))
            link(pool.affine_select(out=ident[:, :], in_=ident[:, :], compare_op=ALU.not_equal, fill=1.0, base=0,
                                    pattern=[[-1, P]], channel_multiplier=1))
            assert done[0] == N_IDENT
            link(pool.iota(expert_noi[:, :], pattern=[[1, E]], base=0, channel_multiplier=0))
            link(pool.iota(tagsi[:, :], pattern=[[2 * P, TILES]], base=-NO_ROW, channel_multiplier=2))
            link(pool.iota(row_noi[:, :], pattern=[[1, 1]], base=0, channel_multiplier=1))
            link(pool.memset(neghalf[:, :], -0.5))
            link(pool.memset(epscol[:, :], EPS))
            assert done[0] == N_SMALL
            pool.wait_ge(id_picked, DEPTH)
            for r in range(DEPTH):
                pool.indirect_dma_start(out=hg[:, r, :], out_offset=None, in_=tok_w[:, :],
                                        in_offset=bass.IndirectOffsetOnAxis(ap=row_id[:, r:r + 1], axis=0)
                                        ).then_inc(gathered[r], 16)
            link(pool.memset(onesb[:, :], 1.0))
            link(pool.affine_select(out=before[:, :], in_=onesb[:, :], compare_op=ALU.is_ge, fill=0.0, base=-1,
                                    pattern=[[1, P]], channel_multiplier=-1))
            assert done[0] == N_POOL_SETUP

            def step(i, u):
                t, q, r = place(i, u, GATHER)
                if live(t) and past(t, DEPTH):
                    pool.wait_ge(id_picked, t + 1)
                    pool.wait_ge(xn_ready, t - DEPTH + 1)
                    pool.wait_ge(res_saved[r], 16 * q)
                t, q, r = place(i, u, SCATTER)
                if live(t):
                    pool.wait_ge(slot_ready, t + 1)
                    if isinstance(t, int) and t == 0:
                        pool.wait_ge(zeroed, 16 * N_ZERO)
                a, _, ar = place(i, u, NORM1)
                b, _, _ = place(i, u, NORM2)
                if live(a) or live(b):
                    lo, hi = (0 if live(a) else 1), (2 if live(b) else 1)
                    if live(a):
                        pool.wait_ge(aggr1, a + 1)
                    if live(b):
                        pool.wait_ge(aggr2, b + 1)
                    pool.tensor_tensor(rs[:, ar % 2, 0, lo:hi], mv[:, ar % 2, lo:hi, 1], epscol[:, lo:hi],
                                       ALU.add).then_inc(var_ready, 1)
                    pool.wait_ge(var_ready, a + 1)
                    pool.tensor_tensor(rs[:, ar % 2, 1, lo:hi], rs[:, ar % 2, 0, lo:hi], neghalf[:, lo:hi],
                                       ALU.pow).then_inc(rstd, 1)
                t, q, r = place(i, u, SCATTER)
                if live(t):
                    pool.wait_ge(rank_done, t + 1)
                    pool.tensor_tensor(count[:, :], count[:, :], pick[:, r % 2, 0, :], ALU.add).then_inc(counted_first, 1)
                    pool.wait_ge(counted_first, t + 1)
                    pool.tensor_tensor(count[:, :], count[:, :], pick[:, r % 2, 1, :], ALU.add).then_inc(counted, 1)
                t, q, r = place(i, u, GATHER)
                if live(t) and past(t, DEPTH):
                    pool.indirect_dma_start(out=hg[:, r, :], out_offset=None, in_=tok_w[:, :],
                                            in_offset=bass.IndirectOffsetOnAxis(ap=row_id[:, r:r + 1], axis=0)
                                            ).then_inc(gathered[r], 16)
                t, q, r = place(i, u, SCATTER)
                if live(t):
                    for k in range(2):
                        pool.indirect_dma_start(out=xslots[:, :],
                                                out_offset=bass.IndirectOffsetOnAxis(ap=slot[:, r, k:k + 1], axis=0),
                                                in_=x2[:, r, :], in_offset=None, bounds_check=SLOTS - 1,
                                                oob_is_err=False).then_inc(scattered[r], 16)

            rounds(pool, step)

            pool.wait_ge(ytok_zeroed, 16 * ZERO_ROUNDS)
            pool.engine_nop().then_inc(held, 1)
            with pool.Fori(0, EPAIRS // DEPTH) as i:
                for r in range(DEPTH):
                    j = DEPTH * i + r
                    pool.wait_ge(held, j + 1)
                    pool.wait_ge(row_ready, j + 1)
                    pool.wait_ge(y_ready, 2 * (j + 1))
                    pool.tensor_tensor(wait_holder[:, :], neghalf[:, 0:1], epscol[:, 0:1], ALU.add).then_inc(held, 1)
                    for n in range(4):
                        pool.indirect_dma_start(out=ytok[:, :],
                                                out_offset=bass.IndirectOffsetOnAxis(ap=row_i[:, r, n:n + 1], axis=0),
                                                in_=ys[:, r, n * P:(n + 1) * P], in_offset=None, bounds_check=NO_ROW - 1,
                                                oob_is_err=False).then_inc(y_out[r], 16)

        @block.tensor
        def _(pe):
            pe.wait_ge(pool_setup, N_IDENT)
            pe.wait_ge(ids_ready, 1)
            pe.transpose(ps[:, 3, 0:TILES], ids_f[:, :], ident[0:TILES, 0:TILES]).then_inc(ids_T, 1)
            pe.wait_ge(weights_in, 16 * N_WEIGHTS)
            for n in range(3):
                pe.transpose(ps[:, 0, n * P:(n + 1) * P], raw[:, n, :], ident[:, :])
            pe.transpose(ps[:, 2, 0:E], raw_gate[:, :], ident[0:E, 0:E])
            pe.wait_ge(wo_ready, 1)
            pe.transpose(ps[:, 1, 0:P], wo_perm[:, :], ident[:, :]).then_inc(setup_T, 1)
            pe.wait_ge(dve_setup, N_DVE_SETUP)
            pe.wait_ge(act_setup, 1)

            pe.wait_ge(xn_ready, 2)

            def score(i, u, half):
                t, q, r = place(i, u, SCORE)
                if not live(t):
                    return
                pe.wait_ge(qk_ready, t + 1)
                if isinstance(t, int) and t == 0:
                    pe.wait_ge(pool_setup, N_POOL_SETUP)
                c = 4 * W
                if r == 0:
                    start = (t % SEQ_TILES == 0) if isinstance(t, int) else (i & 1)
                    c = 4 * W - start * (4 * W)
                pairs = (2 * half, 2 * half + 1)
                for pair in pairs:
                    pe.matmul(S(pair), identb[:, :], masks[:, :, :, :].rearrange("p n w k -> p (n w k)")[:, bass.ds(c, 4 * W)], start=True, stop=False)
                for blk in range(2):
                    last = r if blk else (r - 1) % DEPTH
                    for pair in pairs:
                        rows = slice(32 * pair, 32 * pair + 32)
                        keys = KT[rows, :, :, :].rearrange("p f t k -> p (f t) k")[:, r:DEPTH + last + 1:DEPTH + last - r, :]
                        mm = pe.matmul(S(pair)[:, blk * P:(blk + 1) * P],
                                       QT[rows, r % 2, blk, :, :].rearrange("p a q -> p (a q)"), keys,
                                       start=False, stop=(blk == 1))
                mm.then_inc(s_done[half], 1)

            def turn_probs(t, r, half):
                pe.wait_ge(p_ready[half], t + 1)
                if past(t, 1):
                    pe.wait_ge(pT_ready[half], t)
                for n in range(4):
                    mm = pe.transpose(PT(half)[:, n * P:(n + 1) * P], prob[:, r % 2, half, n * P:(n + 1) * P], ident[:, :])
                mm.then_inc(pT_done[half], 1)

            def step(i, u):
                c, _, cr = place(i, u, PROJ)
                e, _, er = place(i, u, VALUE)
                f, _, fr = place(i, u, OUTP)
                g, _, gr = place(i, u, GATE)
                h, _, hr = place(i, u, ROUTE)

                if live(c - 1):
                    pe.wait_ge(qk_ready, c)
                if live(g - 1):
                    pe.wait_ge(elog_ready, g)
                if live(f):
                    pe.wait_ge(attn_ready, f + 1)
                    for blk in range(2):
                        mm = pe.transpose(p_turn[:, blk * P:(blk + 1) * P], attn[:, fr % 2, blk, :], ident[:, :])
                    mm.then_inc(turn_done, 1)
                if live(c):
                    pe.wait_ge(xn_ready, c + 1)
                    pe.transpose(p_xT, xn[:, cr % 2, :], ident[:, :]).then_inc(xT_done, 1)
                if live(g):
                    pe.wait_ge(x2_ready, g + 1)
                    pe.transpose(p_x2T, x2[:, gr, 0:D], ident[:, :]).then_inc(x2T_done, 1)

                if live(e):
                    if live(c - 1):
                        pe.wait_ge(v_ready, c)
                    turn_probs(e, er, 0)
                score(i, u, 0)

                if live(c):
                    pe.wait_ge(xT_ready, c + 1)
                if live(f) or live(g):
                    pe.wait_ge(mix_ready, f + 1)
                if live(c):
                    cur = xnT[:, cr % 2, :]
                    pe.matmul(p_q, WqT[:, :], cur, start=True, stop=True)
                    pe.matmul(p_k, WkT[:, :], cur, start=True, stop=True).then_inc(qk_done, 1)
                if live(g):
                    pe.matmul(p_log, mixT[:, gr % 2, 1, :], gateT[:, :], start=True, stop=True).then_inc(log_done, 1)

                if live(e):
                    turn_probs(e, er, 1)

                if live(e - 1):
                    pe.wait_ge(attn_ready, e)
                else:
                    if live(f - 1):
                        pe.wait_ge(res_ready, f)
                    if live(h - 1):
                        pe.wait_ge(rank_read, h)
                if live(f):
                    pe.matmul(p_wo, mixT[:, fr % 2, 0, :], WoT[:, :], start=True, stop=True).then_inc(wo_done, 1)
                if live(h):
                    pe.wait_ge(pick_ready, h + 1)
                    if past(h, 1):
                        pe.wait_ge(counted, h)
                    pe.matmul(p_rank, onesb[:, :], base[:, :], start=True, stop=False)
                    pe.matmul(p_rank, onesb[:, :], count[:, :], start=False, stop=False)
                    pe.matmul(p_rank, before[:, :], pick[:, hr % 2, 0, :], start=False, stop=False)
                    pe.matmul(p_rank, before[:, :], pick[:, hr % 2, 1, :], start=False, stop=True).then_inc(rank_done, 1)

                if live(c):
                    if live(e):
                        pe.wait_ge(pT_ready[0], e + 1)
                    pe.matmul(p_v, xnT[:, cr % 2, :], WvT[:, :], start=True, stop=True).then_inc(v_done, 1)

                score(i, u, 1)

                if live(e):
                    if live(f):
                        pe.wait_ge(res_ready, f + 1)
                    if live(h):
                        pe.wait_ge(rank_read, h + 1)
                    pe.wait_ge(v_ready, e + 1)
                    for half in range(2):
                        pe.wait_ge(pT_ready[half], e + 1)
                        for n in range(2):
                            for blk in range(2):
                                pair = 2 * half + n
                                o0 = (blk * PAIRS + pair) * VW
                                k0 = (2 * n + blk) * P
                                mm = pe.matmul(p_o[:, o0:o0 + VW], probT[:, half, k0:k0 + P],
                                               V[:, er, blk, pair * VW:(pair + 1) * VW], start=True, stop=True)
                    mm.then_inc(o_done, 1)

            rounds(pe, step)

            pe.wait_ge(attn_ready, TILES)
            pe.wait_ge(shared_in, 48)
            for b in range(2):
                pe.wait_ge(x2T_saved[b], 16 * (TILES // 2))

            def pair_step(i, u):
                j, q, r = pair_place(i, u, LOAD)
                if pair_live(j):
                    pe.wait_ge(xs_in[r], 16 * (q + 1))
                    if past(j, 2):
                        pe.wait_ge(xsT_ready, j - 1)
                    for s in range(4):
                        mm = pe.transpose(ps[:, r % 2, s * P:(s + 1) * P], xs[:, r, s, 0:D], ident[:, :])
                    mm.then_inc(xsT_done, 1)
                j, q, r = pair_place(i, u, SHARED + 1)
                if pair_live(j):
                    pe.wait_ge(sh_hid_ready, j + 1)
                    for n in range(2):
                        mm = pe.matmul(ps[:, 7, n * P:(n + 1) * P], hid_sh[:, n * P:(n + 1) * P], shared2[:, :],
                                       start=True, stop=True)
                    mm.then_inc(sh_done, 1)
                j, q, r = pair_place(i, u, UP)
                if pair_live(j):
                    pe.wait_ge(w_in[r], 48 * (q + 1))
                    pe.wait_ge(xsT_ready, j + 1)
                    if past(j, 2):
                        pe.wait_ge(hid_ready, j - 1)
                    for s in range(4):
                        mm = pe.matmul(ps[:, 2 + r % 2, s * P:(s + 1) * P], xsT[:, r % 2, s * P:(s + 1) * P],
                                       w13[:, r, s // 2, :, :], start=True, stop=True)
                    mm.then_inc(up_done, 1)
                j, q, r = pair_place(i, u, SHARED)
                if pair_live(j):
                    if past(j, 1):
                        pe.wait_ge(sh_added, j)
                    for n in range(2):
                        mm = pe.matmul(ps[:, 7, n * 2 * P:(n + 1) * 2 * P], shared13[:, n, :], x2T_all[:, tile_cols(j, 2 * P)],
                                       start=True, stop=True)
                    mm.then_inc(sh_up_done, 1)
                j, q, r = pair_place(i, u, TURN)
                if pair_live(j):
                    pe.wait_ge(hid_ready, j + 1)
                    if past(j, 1):
                        pe.wait_ge(hidT_ready, j)
                    for n in range(2):
                        mm = pe.transpose(ps[:, 4, n * P:(n + 1) * P],
                                          hid[:, r % 2, n, :, :].rearrange("p e h -> p (e h)"), ident[:, :])
                    mm.then_inc(hidT_done, 1)
                j, q, r = pair_place(i, u, DOWN)
                if pair_live(j):
                    pe.wait_ge(hidT_ready, j + 1)
                    if past(j, 1):
                        pe.wait_ge(y_ready, 2 * j)
                    for n in range(2):
                        for e in range(2):
                            rows = slice(e * H, (e + 1) * H)
                            c = (r % 2) * 2 * P + n * P
                            mm = pe.matmul(ps[:, 5 + e, c:c + P], hidT[rows, r % 2, n * P:(n + 1) * P],
                                           w2s[rows, r, :], start=True, stop=True)
                    mm.then_inc(y_done, 1)

            pair_rounds(pe, pair_step, SHARED + 2)

        @block.vector
        def _(dve):
            done = [0]

            def mark(ins):
                done[0] += 1
                ins.then_inc(dve_setup, 1)

            def link(ins):
                mark(ins)
                dve.wait_ge(dve_setup, done[0])

            dve.wait_ge(ids_in, 16)
            dve.tensor_copy(ids_f[:, :], ids_i[:, :]).then_inc(ids_ready, 1)
            dve.wait_ge(ids_T, 1)
            mark(dve.tensor_copy(idsT[:, :], ps[:, 3, 0:TILES]))
            dve.tensor_copy(row_id[:, :], ps[:, 3, 0:DEPTH]).then_inc(id_picked, DEPTH)
            dve.wait_ge(weights_in, 16 * N_WEIGHTS)
            dve.tensor_copy(wo_perm[:, :].rearrange("o (a b d) -> o a b d", a=2, b=PAIRS),
                            raw[:, 3, :].rearrange("o (b a d) -> o a b d", a=2, b=PAIRS)).then_inc(wo_ready, 1)
            mark(dve.memset(V[:, :, :, :].rearrange("p t b (g c) -> p (t b g) c", c=VW)[:, :, 2 * HD:VW], 1.0))
            mark(dve.memset(V[W:P, 0, 0, :].rearrange("p (g c) -> p g c", c=VW)[:, :, 0:2 * HD], 0.0))
            mark(dve.memset(KT[:, 1, DEPTH - 1, :], 0.0))
            mark(dve.memset(tags[:, :], 0.0))
            mark(dve.memset(limit[:, 0:1], 0.0))
            mark(dve.memset(x2[:, :, D:ROW], 0.0))
            mark(dve.memset(count[:, :], 0.0))
            link(dve.memset(base[:, :], 0.0))
            dve.wait_ge(setup_T, 1)
            mark(dve.tensor_copy(gateT[:, :], ps[:, 2, 0:E]))
            mark(dve.tensor_copy(WoT[:, :], ps[:, 1, 0:P]))
            mark(dve.tensor_copy(identb[:, :], ident[:, :]))
            view = ident[:, :].rearrange("p (g c) -> p g c", c=2 * HD)
            for a in range(2):
                mark(dve.tensor_reduce(qscale[:, a:a + 1], view[:, :, a * HD:(a + 1) * HD], AX.XY, ALU.add))
            dve.wait_ge(pool_setup, N_SMALL)
            link(dve.tensor_scalar(limit_of[:, :], expert_noi[:, :], float(CAP), float(CAP), ALU.mult, ALU.add))
            mark(dve.tensor_copy(key_no[:, :], expert_noi[:, :]))
            link(dve.tensor_copy(row_no[:, :], row_noi[:, :]))
            link(dve.tensor_scalar(query[:, :], row_no[:, :], float(W), -float(W), ALU.is_ge, ALU.mult))
            link(dve.tensor_tensor(query[:, :], query[:, :], row_no[:, :], ALU.add))
            keys = key_no[:, :].unsqueeze(1).unsqueeze(1).to_broadcast([P, 2, 2, W])
            for c, masked_if in ((slice(0, 4, 3), ALU.is_gt), (slice(1, 3), ALU.is_le)):
                ins = dve.tensor_scalar(masks[:, :, c, :], keys, query[:, 0:1], MASKED, masked_if, ALU.mult)
            link(ins)
            mark(dve.memset(masks[:, 0, 1, :], MASKED))
            mark(dve.tensor_scalar(qscale[:, :], qscale[:, :], -SCALE, None, ALU.mult))
            mark(dve.tensor_copy(limit_at[:, :, :], limit_of[:, :].unsqueeze(2).to_broadcast([P, E, 2])))
            mark(dve.tensor_copy(tags[:, :].rearrange("p (t k) -> p t k", k=2)[:, :, 0], tagsi[:, :]))
            mark(dve.tensor_scalar(base[0:1, :], limit_of[0:1, :], float(CAP), None, ALU.subtract))
            for a in range(2):
                mark(dve.memset(attn[a * W:(a + 1) * W, :, :, (1 - a) * W:(2 - a) * W], 0.0))
            link(dve.memset(warm[:, :], 0.0))
            dve.memset(zeros[:, :], 0.0).then_inc(consts_ready, 1)
            assert done[0] == N_DVE_SETUP, done[0]

            def row_low(t, r, half):
                if live(t):
                    dve.wait_ge(s_done[half], t + 1)
                    scores = ps[:, 2 * half:2 * half + 2, 0:2 * P].rearrange("p n (b k) -> p n b k", b=2)
                    dve.tensor_reduce(low[:, r % 2, 2 * half:2 * half + 2, :], scores, AX.X, ALU.min
                                      ).then_inc(low_ready[half], 1)

            def step(i, u):
                gt, gq, gr = place(i, u, GATHER)
                at, aq, ar = place(i, u, NORM1)
                bt, _, _ = place(i, u, NORM2)
                et, _, er = place(i, u, ATTN)
                t, q, r = place(i, u, ROUTE)
                b = r % 2
                ab = ar % 2
                if live(gt) and past(gt, DEPTH):
                    dve.wait_ge(gathered[gr], 16 * gq)
                    dve.tensor_copy(row_id[:, gr:gr + 1], idsT[:, bass.ds(gt, 1)]).then_inc(id_picked, 1)
                if live(at):
                    dve.wait_ge(gathered[ar], 16 * (aq + 1))
                if live(bt):
                    dve.wait_ge(res_ready, bt + 1)
                if live(t):
                    dve.wait_ge(elog_ready, t + 1)
                    dve.tensor_scalar(negd[:, :], elog[:, b, :], -1.0, -1.0, ALU.mult, ALU.add).then_inc(negd_ready, 1)
                if live(at):
                    dve.bn_stats(st1[:, :], hg[:, ar, :]).then_inc(stats1, 1)
                if live(bt):
                    dve.bn_stats(st2[:, :], hres[:, tile_cols(bt)]).then_inc(stats2, 1)
                    dve.wait_ge(stats2, bt + 1)
                if live(at):
                    dve.wait_ge(stats1, at + 1)
                if live(t):
                    dve.wait_ge(negd_ready, t + 1)
                if live(et):
                    dve.wait_ge(o_done, et + 1)
                    o = p_o.rearrange("p (b g c) -> p b g c", b=2, c=VW)
                    rr = rsum[:, er % 2, :].rearrange("p (b g) -> p b g", b=2)
                    dve.reciprocal(rr, o[:, :, :, 2 * HD]).then_inc(rsum_ready, 1)
                if live(at):
                    dve.bn_aggr(mv[:, ab, 0, :], st1[:, :]).then_inc(aggr1, 1)
                if live(bt):
                    dve.bn_aggr(mv[:, ab, 1, :], st2[:, :]).then_inc(aggr2, 1)
                if live(t):
                    dve.max(top[:, :], negd[:, :]).then_inc(top_ready, 1)
                if live(et):
                    dve.wait_ge(rsum_ready, et + 1)
                    if past(et, 2):
                        dve.wait_ge(turn_done, et - 1)
                    for a in range(2):
                        rows = slice(a * W, (a + 1) * W)
                        ins = dve.tensor_tensor(
                            attn[rows, er % 2, :, a * W:(a + 1) * W].rearrange("p b (g d) -> p b g d", d=HD),
                            o[rows, :, :, a * HD:(a + 1) * HD],
                            rr[rows].unsqueeze(3).to_broadcast([W, 2, PAIRS, HD]), ALU.mult)
                    ins.then_inc(attn_ready, 1)
                if live(t):
                    dve.wait_ge(top_ready, t + 1)
                    dve.tensor_copy(top_all[:, tile_cols(t, 2)], top[:, 0:2]).then_inc(top_saved, 1)
                    dve.max_index(topi[:, :], top[:, :], negd[:, :]).then_inc(topi_ready, 1)
                    dve.wait_ge(topi_ready, t + 1)
                    dve.tensor_scalar(limit[:, 1:3], topi[:, 0:2], float(CAP), float(CAP), ALU.mult, ALU.add).then_inc(limit_ready, 1)
                    dve.wait_ge(limit_ready, t + 1)
                    if past(t, 2):
                        dve.wait_ge(counted, t - 1)
                    dve.tensor_tensor(pick[:, b, :, :], limit_of[:, :].unsqueeze(1).to_broadcast([P, 2, E]),
                                      limit[:, 1:3].unsqueeze(2).to_broadcast([P, 2, E]), ALU.is_equal).then_inc(pick_ready, 1)
                st, _, sr = place(i, u, SCORE)
                row_low(st, sr, 0)
                t, q, r = place(i, u, NORM1)
                if live(t):
                    dve.wait_ge(rstd, t + 1)
                    if past(t, 2):
                        dve.wait_ge(xT_done, t - 1)
                    dve.tensor_scalar(xn[:, r % 2, :], hg[:, r, :], mv[:, r % 2, 0, 0:1], rs[:, r % 2, 1, 0:1], ALU.subtract,
                                      ALU.mult).then_inc(xn_ready, 1)
                t, q, r = place(i, u, NORM2)
                if live(t):
                    dve.wait_ge(rstd, t + NORM2 - NORM1 + 1)
                    if past(t, DEPTH):
                        dve.wait_ge(x2T_done, t - DEPTH + 1)
                        dve.wait_ge(scattered[r], 32 * q)
                    dve.tensor_scalar(x2[:, r, 0:D], hres[:, tile_cols(t)], mv[:, r % 2, 1, 0:1], rs[:, r % 2, 1, 1:2], ALU.subtract,
                                      ALU.mult).then_inc(x2_ready, 1)
                h, _, hr = place(i, u, ROUTE)
                t, q, r = place(i, u, OUTP)
                if live(h):
                    dve.wait_ge(rank_done, h + 1)
                if live(t):
                    dve.wait_ge(wo_done, t + 1)
                    dve.wait_ge(res_saved[r], 16 * (q + 1))
                    dve.tensor_tensor(hres[:, tile_cols(t)], p_wo, hres[:, tile_cols(t)], ALU.add).then_inc(res_ready, 1)
                if live(h):
                    dve.tensor_tensor(rank[:, :, :], p_rank.unsqueeze(1).to_broadcast([P, 2, E]), pick[:, hr % 2, :, :],
                                      ALU.mult).then_inc(rank_read, 1)
                    dve.wait_ge(rank_read, h + 1)
                    dve.tensor_reduce(seat[:, :], rank[:, :, :], AX.X, ALU.add).then_inc(seat_ready, 1)
                    dve.wait_ge(seat_ready, h + 1)
                    dve.tensor_tensor(over[:, :], seat[:, :], limit[:, 1:3], ALU.is_ge).then_inc(over_ready, 1)
                    dve.tensor_tensor(x2[:, hr, D:D + 2], tags[:, tile_cols(h, 2)], limit[:, 0:2], ALU.add)
                    dve.wait_ge(over_ready, h + 1)
                    dve.scalar_tensor_tensor(slot[:, hr, :], over[:, :], float(2 * SLOTS), seat[:, :], ALU.mult,
                                             ALU.add).then_inc(slot_ready, 1)
                row_low(st, sr, 1)

            rounds(dve, step)

            dve.wait_ge(top_saved, TILES)
            dve.reciprocal(best_all[:, :], top_all[:, :]).then_inc(gains, 1)
            dve.wait_ge(gains, 1)
            best = best_all[:, :].rearrange("p (t k) -> p t k", k=2)
            dve.scalar_tensor_tensor(sum_all[:, :], best[:, :, 0], -1e-20, best[:, :, 1], ALU.add, ALU.add).then_inc(gains, 1)
            dve.wait_ge(gains, 2)
            dve.reciprocal(inv_all[:, :], sum_all[:, :]).then_inc(gains, 1)
            dve.wait_ge(gains, 3)
            dve.scalar_tensor_tensor(gain_all[:, :].rearrange("p (t k) -> p t k", k=2), best, ROUTE_SCALE,
                                     inv_all[:, :].unsqueeze(2).to_broadcast([P, TILES, 2]), ALU.mult, ALU.mult
                                     ).then_inc(gains, 1)
            dve.wait_ge(gains, 4)

            limit_at_flat = limit_at[:, :, :].rearrange("p e i -> p (e i)")

            def pair_step(i, u):
                j, q, r = pair_place(i, u, LOAD)
                if pair_live(j):
                    dve.wait_ge(xs_in[r], 16 * (q + 1))
                    dve.tensor_tensor(other[:, r, :], xs[:, r, :, D + 1], limit_at_flat[:, tile_cols(j, 4)],
                                      ALU.not_equal).then_inc(other_ready, 1)
                j, q, r = pair_place(i, u, SHARED + 1)
                if pair_live(j):
                    dve.wait_ge(sh_done, j + 1)
                    dve.tensor_tensor(hres[:, tile_cols(j, 2 * P)], ps[:, 7, 0:2 * P], hres[:, tile_cols(j, 2 * P)],
                                      ALU.add).then_inc(sh_added, 1)
                j, q, r = pair_place(i, u, LOAD)
                if pair_live(j):
                    dve.wait_ge(other_ready, j + 1)
                    dve.scalar_tensor_tensor(row_f[:, r, :], other[:, r, :], float(NO_ROW), xs[:, r, :, D], ALU.add,
                                             ALU.add).then_inc(tags_read, 1)
                j, q, r = pair_place(i, u, UP)
                if pair_live(j):
                    b = r % 2
                    up = ps[:, 2 + b, :].rearrange("p (s a h) -> p s a h", s=4, a=2)
                    dve.wait_ge(silu_ready, j + 1)
                    if past(j, 2):
                        dve.wait_ge(hidT_done, j - 1)
                    dve.tensor_tensor(hid[:, b, :, :, :].rearrange("p n e h -> p e n h"),
                                      up[:, :, 1, :].rearrange("p (e n) h -> p e n h", e=2),
                                      silu[:, b, :, :].rearrange("p (e n) h -> p e n h", e=2),
                                      ALU.mult).then_inc(hid_ready, 1)
                j, q, r = pair_place(i, u, SHARED)
                if pair_live(j):
                    dve.wait_ge(sh_silu_ready, j + 1)
                    dve.tensor_tensor(hid_sh[:, :], ps[:, 7, 2 * P:4 * P], silu_sh[:, :], ALU.mult).then_inc(sh_hid_ready, 1)
                j, q, r = pair_place(i, u, DOWN)
                if pair_live(j):
                    dve.wait_ge(tags_read, j + 1)
                    if past(j, DEPTH):
                        dve.wait_ge(y_out[r], 64 * q)
                    dve.tensor_copy(row_i[:, r, :], row_f[:, r, :]).then_inc(row_ready, 1)
                    dve.wait_ge(y_done, j + 1)
                    dve.tensor_copy(ys[:, r, 0:2 * P], ps[:, 5, (r % 2) * 2 * P:(r % 2 + 1) * 2 * P]).then_inc(y_ready, 1)

            pair_rounds(dve, pair_step, SHARED + 2)

            dve.wait_ge(sh_added, EPAIRS)
            with dve.Fori(0, GROUPS // DEPTH) as i:
                for r in range(DEPTH):
                    g = DEPTH * i + r
                    dve.wait_ge(y_in[r], 16 * (i + 1))
                    for n in range(DEPTH):
                        t = DEPTH * g + n
                        ins = dve.scalar_tensor_tensor(hres[:, tile_cols(t)], ysel[:, r, n, 0:P], gain_all[:, bass.ds(2 * t, 1)],
                                                       hres[:, tile_cols(t)], ALU.mult, ALU.add)
                    ins.then_inc(first_added, 1)
                    dve.wait_ge(first_added, g + 1)
                    dve.wait_ge(scaled, g + 1)
                    rows = hres[:, tile_cols(g, DEPTH * P)].rearrange("p (n d) -> p n d", d=D)
                    dve.tensor_tensor(rows, ysel[:, r, :, P:2 * P], rows, ALU.add).then_inc(complete, 1)

        @block.scalar
        def _(act):
            act.wait_ge(setup_T, 1)
            for n, wT in enumerate((WqT, WkT, WvT)):
                ins = act.copy(wT[:, :], ps[:, 0, n * P:(n + 1) * P])
            ins.then_inc(act_setup, 1)
            act.wait_ge(dve_setup, N_DVE_SETUP)

            def exps(t, r, half):
                if live(t):
                    act.wait_ge(low_ready[half], t + 1)
                    for n in range(2):
                        pair = 2 * half + n
                        for blk in range(2):
                            k0 = (2 * n + blk) * P
                            ins = act.activation(prob[:, r % 2, half, k0:k0 + P], S(pair)[:, blk * P:(blk + 1) * P], ACT.Exp,
                                                 bias=low[:, r % 2, pair, blk:blk + 1], scale=-1.0)
                    ins.then_inc(p_ready[half], 1)

            def copy_pT(i, u, half):
                t, q, r = place(i, u, VALUE)
                if live(t):
                    act.wait_ge(pT_done[half], t + 1)
                    if past(t, 1):
                        act.wait_ge(o_done, t)
                    act.copy(probT[:, half, :], PT(half)).then_inc(pT_ready[half], 1)

            def step(i, u):
                c, _, cr = place(i, u, PROJ)
                d, _, dr = place(i, u, SCORE)
                e, _, er = place(i, u, VALUE)
                f, _, fr = place(i, u, OUTP)
                g, gq, gr = place(i, u, GATE)
                if live(c):
                    act.wait_ge(xT_done, c + 1)
                    if past(c, 1):
                        act.wait_ge(v_done, c)
                        act.wait_ge(qk_done, c)
                if live(f):
                    act.wait_ge(turn_done, f + 1)
                    if past(f, 2):
                        act.wait_ge(wo_done, f - 1)
                if live(g):
                    act.wait_ge(x2T_done, g + 1)
                    if past(g, 2):
                        act.wait_ge(log_done, g - 1)
                        act.wait_ge(x2T_saved[gr % 2], 16 * (2 * gq + gr // 2))
                if live(c):
                    act.copy(xnT[:, cr % 2, :], p_xT).then_inc(xT_ready, 1)
                if live(f) or live(g):
                    ins = None
                    if live(f):
                        for a in range(2):
                            rows = slice(a * W, (a + 1) * W)
                            ins = act.copy(mixT[rows, fr % 2, 0, :].rearrange("p (b q) -> p b q", b=2),
                                           p_turn[rows].rearrange("p (b a q) -> p b a q", b=2, a=2)[:, :, a, :])
                    if live(g):
                        ins = act.copy(mixT[:, fr % 2, 1, :], p_x2T)
                    ins.then_inc(mix_ready, 1)
                copy_pT(i, u, 0)
                exps(d, dr, 0)
                copy_pT(i, u, 1)
                if live(g):
                    act.wait_ge(log_done, g + 1)
                    if past(g, 2):
                        act.wait_ge(negd_ready, g - 1)
                if live(c):
                    act.wait_ge(qk_done, c + 1)
                    if past(c, 2):
                        act.wait_ge(s_done[1], c - 1)
                    for a in range(2):
                        act.activation(QT[:, cr % 2, :, a, :], p_q.rearrange("p (b q) -> p b q", b=2), ACT.Identity,
                                       scale=qscale[:, a:a + 1])
                    act.copy(KT[:, :, cr, :], p_k.rearrange("p (f k) -> p f k", f=2)).then_inc(qk_ready, 1)
                if live(g):
                    act.activation(elog[:, gr % 2, :], p_log, ACT.Exp, scale=-1.0).then_inc(elog_ready, 1)
                if live(c):
                    act.wait_ge(v_done, c + 1)
                    if past(c, DEPTH - 1):
                        act.wait_ge(o_done, c - DEPTH + 2)
                    for rows, r, blk in ((slice(0, P), cr, 1), (slice(0, W), cr, 0), (slice(W, P), (cr + 1) % DEPTH, 0)):
                        ins = act.copy(V[rows, r, blk, :].rearrange("p (g c) -> p g c", c=VW)[:, :, 0:2 * HD],
                                       p_v[rows].rearrange("p (g c) -> p g c", c=2 * HD))
                    ins.then_inc(v_ready, 1)

                exps(d, dr, 1)

            rounds(act, step)
            act.activation(warm[:, :], warm[:, :], ACT.Silu)

            def pair_step(i, u):
                j, q, r = pair_place(i, u, LOAD)
                if pair_live(j):
                    act.wait_ge(xsT_done, j + 1)
                    if past(j, 2):
                        act.wait_ge(up_done, j - 1)
                    act.copy(xsT[:, r % 2, :], ps[:, r % 2, :]).then_inc(xsT_ready, 1)
                j, q, r = pair_place(i, u, UP)
                if pair_live(j):
                    act.wait_ge(up_done, j + 1)
                    if past(j, 2):
                        act.wait_ge(hid_ready, j - 1)
                    act.activation(silu[:, r % 2, :, :],
                                   ps[:, 2 + r % 2, :].rearrange("p (s a h) -> p s a h", s=4, a=2)[:, :, 0, :],
                                   ACT.Silu).then_inc(silu_ready, 1)
                j, q, r = pair_place(i, u, SHARED)
                if pair_live(j):
                    act.wait_ge(sh_up_done, j + 1)
                    if past(j, 1):
                        act.wait_ge(sh_hid_ready, j)
                    act.activation(silu_sh[:, :], ps[:, 7, 0:2 * P], ACT.Silu).then_inc(sh_silu_ready, 1)
                j, q, r = pair_place(i, u, TURN)
                if pair_live(j):
                    act.wait_ge(hidT_done, j + 1)
                    if past(j, 2):
                        act.wait_ge(y_done, j - 1)
                    act.copy(hidT[:, r % 2, :], ps[:, 4, 0:2 * P]).then_inc(hidT_ready, 1)
                j, q, r = pair_place(i, u, DOWN)
                if pair_live(j):
                    act.wait_ge(y_done, j + 1)
                    if past(j, DEPTH):
                        act.wait_ge(y_out[r], 64 * q)
                    act.copy(ys[:, r, 2 * P:4 * P], ps[:, 6, (r % 2) * 2 * P:(r % 2 + 1) * 2 * P]).then_inc(y_ready, 1)

            pair_rounds(act, pair_step, SHARED + 2)

            act.wait_ge(gains, 4)
            with act.Fori(0, GROUPS // DEPTH) as i:
                for r in range(DEPTH):
                    act.wait_ge(y_in[r], 16 * (i + 1))
                    for n in range(DEPTH):
                        t = DEPTH * (DEPTH * i + r) + n
                        ins = act.activation(ysel[:, r, n, P:2 * P], ysel[:, r, n, P:2 * P], ACT.Identity,
                                             scale=gain_all[:, bass.ds(2 * t + 1, 1)])
                    ins.then_inc(scaled, 1)


_INS = ['x', 'L0_tok_w', 'L0_attn_Wq', 'L0_attn_Wk', 'L0_attn_Wv', 'L0_attn_Wo', 'L0_ffn_gate_w', 'L0_ffn_w1',
        'L0_ffn_w3', 'L0_ffn_w2', 'L0_ffn_sw1', 'L0_ffn_sw3', 'L0_ffn_sw2']
_OUTS = [((8, 1024, 128), 'float32')]


def kernel(**inputs):
    import numpy as _np
    import concourse.bacc as _bacc
    from concourse import mybir as _mybir
    from concourse.bass_utils import run_bass_kernel_spmd as _run

    nc = _bacc.Bacc("TRN2", target_bir_lowering=False, num_devices=1)
    arrays, args = {}, []
    for name in _INS:
        a = _np.ascontiguousarray(inputs[name])
        arrays[f"in_{name}_dram"] = a
        args.append(nc.dram_tensor(f"in_{name}_dram", a.shape, _mybir.dt.from_np(a.dtype), kind="ExternalInput").ap())
    for i, (shape, dtype) in enumerate(_OUTS):
        dt = _mybir.dt.from_np(_np.dtype(dtype))
        args.append(nc.dram_tensor(f"out_{i}_dram", shape, dt, kind="ExternalOutput").ap())
    lm_tower(nc, *args)
    r = _run(nc, [arrays], core_ids=[0])
    return r.results[0]["out_0_dram"]
```
